# Optimizing a Trainium2 kernel written in Bass

```python
import numpy as np
import jax
import jax.numpy as jnp

def _softmax(x, axis=-1):
    return jax.nn.softmax(x, axis=axis)
def _gelu(x):
    return jax.nn.gelu(x, approximate=True)
def _silu(x):
    return jax.nn.silu(x)
def _sigmoid(x):
    return jax.nn.sigmoid(x)
def _layernorm(x, axis=-1, eps=1e-5):
    m = jnp.mean(x, axis=axis, keepdims=True)
    v = jnp.var(x, axis=axis, keepdims=True)
    return (x - m) / jnp.sqrt(v + eps)
def _scatter_add(tgt, idx, src, axis=0):
    return tgt.at[idx].add(src)
def _segment_sum(src, seg, n):
    return jax.ops.segment_sum(src, seg, n)

kernel_name = 'mk_adj_resnorm_d1_adj_256_312fcc'

def setup_inputs(seed: int = 0):
    np.random.seed(seed)
    _w = jnp.asarray
    def _rec_inputs():
        import jax
        import jax.numpy as jnp
        _gk = jax.random.key(seed)
        x = -0.0005207 + 1.001 * jax.random.normal(jax.random.fold_in(_gk, 1), (8192, 256), jnp.float32)
        _w = (1.0 + jnp.arange(8192, dtype=jnp.float32)) ** -0.5
        _w = _w / _w.mean()
        _pij = jnp.clip(0.00390625 * _w[:, None] * _w[None, :], 0.0, 1.0)
        _a = jax.random.uniform(jax.random.fold_in(_gk, 2), (8192, 8192)) < _pij
        adj = _a.astype(jnp.int32)
        return x, adj
    x, adj = _rec_inputs()
    def _L0_gnn_setup():
        import jax, jax.numpy as jnp
        import numpy as np
        N_NODES = 8192
        IN_F = 256
        OUT_F = 256
        ALPHA = 0.2
        key = jax.random.key(seed)
        k1, k2, k3, k4 = jax.random.split(key, 4)
        X = jax.random.normal(k1, (N_NODES, IN_F), dtype=jnp.float32)
        A = jax.random.randint(k2, (N_NODES, N_NODES), 0, 2, dtype=jnp.int32)
        W = jax.random.normal(k3, (OUT_F, IN_F), dtype=jnp.float32) * (1.0 / np.sqrt(IN_F))
        r = jax.random.normal(k4, (2 * OUT_F, 1), dtype=jnp.float32)
        return {'X': X, 'A': A, 'W': W, 'r': r}
    _L0_gnn_all = _L0_gnn_setup()
    _L0_gnn_in = {k: v for k, v in _L0_gnn_all.items() if k in ('W', 'r', )}
    del _L0_gnn_all

    return {
        "x": x,
        "adj": adj,
        "L0_gnn_W": _L0_gnn_in["W"],
        "L0_gnn_r": _L0_gnn_in["r"],
    }

def reference(x, adj, L0_gnn_W, L0_gnn_r):
    import jax
    import jax.numpy as jnp
    def _L0_gnn_ref(X, A, W, r):
        import jax, jax.numpy as jnp
        import numpy as np
        N_NODES = 8192
        IN_F = 256
        OUT_F = 256
        ALPHA = 0.2
        Wh = X @ W.T
        F_out = Wh.shape[-1]
        r_src = r[:F_out, 0]
        r_dst = r[F_out:, 0]
        s_i = Wh @ r_src
        s_j = Wh @ r_dst
        e = s_i[:, None] + s_j[None, :]
        e = jnp.where(e >= 0, e, ALPHA * e)
        e = jnp.where(A == 0, -jnp.inf, e)
        attention = jax.nn.softmax(e, axis=1)
        output = attention @ Wh
        return jax.nn.gelu(output, approximate=False)

    x = _layernorm(x + _L0_gnn_ref(x, adj, L0_gnn_W, L0_gnn_r), axis=-1)
    return x


_drawn_inputs = setup_inputs


def setup_inputs(seed=0):
    import zlib

    import numpy as np

    out = dict(_drawn_inputs(seed))
    spreads = {}
    factors = {}
    for name, (base, spread) in spreads.items():
        noise = np.random.default_rng([zlib.crc32(name.encode()), seed]).standard_normal(out[name].shape)
        drawn = base * np.exp(spread * noise) if base else spread * noise
        out[name] = jnp.asarray(drawn.astype(out[name].dtype))
    for name, factor in factors.items():
        out[name] = (out[name] * factor).astype(out[name].dtype)
    return out
```

```python
import concourse.bass as bass
from concourse import mybir
from contextlib import ExitStack

F32 = mybir.dt.float32
I32 = mybir.dt.int32
ALU = mybir.AluOpType
ACT = mybir.ActivationFunctionType
AX = mybir.AxisListType

P = 128
ALPHA = 0.2
EPS = 1e-5
BANK = 512


def general_path(nc, x, adj, W, r, out, taken=None):
    N, FIN = x.shape
    FOUT = W.shape[0]
    NT = N // P
    KT = FIN // P
    OT = FOUT // P
    GRP = BANK // P
    NG = NT // GRP

    ctx = ExitStack()
    with ctx:
        def sb(name, shape, dt=F32):
            return ctx.enter_context(nc.sbuf_tensor("g_" + name, shape, dt))

        def pb(name, shape):
            return ctx.enter_context(nc.psum_tensor("g_" + name, shape, F32))

        def sem(name):
            return ctx.enter_context(nc.semaphore("g_" + name))

        ident = sb("ident", [P, P])
        ones = sb("ones", [P, P])
        w_in = sb("w_in", [P, OT, FIN])
        r_in = sb("r_in", [P, 2 * OT])
        w_ext = sb("w_ext", [P, KT, FOUT + 2])
        x_in = sb("x_in", [P, FIN])
        xT = sb("xT", [P, KT, P])
        Wh = sb("Wh", [P, NT, FOUT + 1])
        S = sb("S", [P, NT, 2])
        diag = sb("diag", [P, P])
        s_row = sb("s_row", [P, N])
        s_min = sb("s_min", [P, 1])
        A = sb("A", [P, N], I32)
        E = sb("E", [P, N])
        row_max = sb("row_max", [P, 3])
        ET = sb("ET", [P, 2, BANK])
        den = sb("den", [P, 1])
        xres = sb("xres", [P, FIN])
        h = sb("h", [P, FOUT])
        y = sb("y", [P, FOUT])
        o = sb("o", [P, FOUT])
        mv = sb("mv", [P, 2])
        rstd = sb("rstd", [P, 1])
        expo = sb("expo", [P, 1])
        ps_t = [pb(f"ps_t{i}", [P, BANK]) for i in range(2)]
        ps_a = pb("ps_a", [P, BANK])
        ps_b = pb("ps_b", [P, BANK])

        s_w = sem("w_loaded")
        s_const = sem("const_ready")
        s_wT = sem("w_transposed")
        s_wTc = sem("w_copied")
        s_wr = sem("w_r_product")
        s_ext = sem("w_ext_ready")
        s_x = sem("x_loaded")
        s_xT = sem("x_transposed")
        s_xTc = sem("x_copied")
        s_wh = sem("wh_product")
        s_whc = sem("wh_stored")
        s_dg = sem("diag_ready")
        s_bc = sem("row_broadcast")
        s_row_ok = sem("row_stored")
        s_dve = sem("vector_step")
        s_adj = sem("adj_loaded")
        s_lg = sem("logits_ready")
        s_exp = sem("exp_done")
        s_pm = sem("weights_masked")
        s_tr = sem("weights_transposed")
        s_cp = sem("transposed_copied")
        s_mm = sem("product_done")
        s_xr = sem("xres_loaded")
        s_h = sem("h_ready")
        s_g = sem("gelu_done")
        s_y = sem("variance_ready")
        s_rs = sem("rstd_ready")
        s_o = sem("out_ready")
        s_st = sem("out_stored")
        block = ctx.enter_context(nc.Block())

        def branch(eng, body):
            if taken is None:
                body()
            else:
                flag = eng.value_load(taken[0:1, 0:1], min_val=0, max_val=1)
                with eng.If(flag == 0):
                    body()

        @block.sync
        def _(sp):
            def body():
                for count in (s_st,):
                    sp.sem_inc(count, 1)
                sp.dma_start(w_in[:], W.rearrange("(t p) k -> p t k", p=P)).then_inc(s_w, 16)
                sp.dma_start(r_in[:], r.rearrange("(u p) a -> p (u a)", p=P),
                             allow_slow_non_contiguous=True).then_inc(s_w, 16)
                with sp.Fori(0, NT) as t:
                    sp.wait_ge(s_xT, t + 1)
                    sp.dma_start(x_in[:], x[bass.ts(t, P), :]).then_inc(s_x, 16)
                with sp.Fori(0, NT) as t:
                    sp.wait_ge(s_pm, t + 1)
                    sp.dma_start(A[:], adj[bass.ts(t, P), :]).then_inc(s_adj, 16)
                    sp.wait_ge(s_o, t + 1)
                    sp.dma_start(xres[:], x[bass.ts(t, P), :]).then_inc(s_xr, 16)
                    sp.wait_ge(s_o, t + 1 + 1)
                    sp.dma_start(out[bass.ts(t, P), :], o[:]).then_inc(s_st, 16)
                sp.wait_ge(s_st, 16 * NT + 1)
            branch(sp, body)

        @block.gpsimd
        def _(pool):
            def body():
                nc.gpsimd.memset(ident[:], 0.0).then_inc(s_const, 1)
                nc.gpsimd.memset(ones[:], 1.0).then_inc(s_const, 1)
                nc.gpsimd.memset(expo[:], -0.5).then_inc(s_const, 1)
                nc.gpsimd.memset(Wh[:, :, FOUT:FOUT + 1], 1.0).then_inc(s_const, 1)
                pool.wait_ge(s_const, 4)
                nc.gpsimd.affine_select(out=ident[:], in_=ident[:], compare_op=ALU.not_equal, fill=1.0,
                                        base=0, pattern=[[-1, P]], channel_multiplier=1).then_inc(s_const, 1)
                with pool.Fori(0, NT) as t:
                    pool.wait_ge(s_y, t + 1)
                    nc.gpsimd.tensor_tensor(rstd[:], mv[:, 1:2], expo[:], ALU.pow).then_inc(s_rs, 1)
            branch(pool, body)

        @block.scalar
        def _(act):
            def body():
                for count in (s_whc, s_row_ok, s_cp,):
                    act.sem_inc(count, 1)
                for g in range(KT):
                    act.wait_ge(s_wT, g + 1)
                    nc.scalar.copy(w_ext[:, g, 0:FOUT], ps_t[g % 2][:, 0:FOUT]).then_inc(s_wTc, 1)
                act.wait_ge(s_wr, 1)
                nc.scalar.copy(w_ext[:, :, FOUT:FOUT + 2],
                               ps_a[:, 0:2 * KT].rearrange("p (k c) -> p k c", c=2)).then_inc(s_ext, 1)
                with act.Fori(0, NT) as t:
                    act.wait_ge(s_xT, t + 1 + 1)
                    nc.scalar.copy(xT[:], ps_t[0][:, 0:FIN].rearrange("p (k m) -> p k m", m=P)).then_inc(s_xTc, 1)
                    act.wait_ge(s_wh, t + 1)
                    nc.scalar.copy(Wh[:, t, 0:FOUT], ps_a[:, 0:FOUT])
                    nc.scalar.copy(S[:, t, :], ps_a[:, FOUT:FOUT + 2]).then_inc(s_whc, 1)
                with act.Fori(0, NT) as t:
                    act.wait_ge(s_bc, t + 1 + 1)
                    nc.scalar.copy(s_row[:, bass.ts(t, P)], ps_b[:, 0:P]).then_inc(s_row_ok, 1)
                with act.Fori(0, NT) as t:
                    act.wait_ge(s_lg, t + 1)
                    nc.scalar.activation(E[:], E[:], ACT.Exp).then_inc(s_exp, 1)
                    for g in range(NG):
                        act.wait_ge(s_tr, NG * t + (g + 1) + 1)
                        if g >= 2:
                            act.wait_ge(s_mm, NG * t + (g - 1))
                        nc.scalar.copy(ET[:, g % 2, :], ps_t[g % 2][:]).then_inc(s_cp, 1)
                    act.wait_ge(s_h, t + 1 + 1)
                    nc.scalar.activation(y[:], h[:], ACT.Gelu).then_inc(s_g, 1)
            branch(act, body)

        @block.vector
        def _(dve):
            def body():
                for count in (s_pm, s_h, s_o,):
                    dve.sem_inc(count, 1)
                with dve.Fori(0, NT) as t:
                    dve.wait_ge(s_const, 5)
                    dve.wait_ge(s_whc, NT + 1)
                    dve.wait_ge(s_bc, t + 1)
                    nc.vector.tensor_scalar(diag[:], ident[:], S[:, t, 1:2], None, ALU.mult).then_inc(s_dg, 1)
                dve.wait_ge(s_row_ok, NT + 1)
                nc.vector.tensor_reduce(s_min[:], s_row[:], AX.X, ALU.min).then_inc(s_dve, 1)
                dve.wait_ge(s_dve, 1)
                with dve.Fori(0, NT) as t:
                    STEPS = 14
                    count = [0]

                    def link(ins):
                        count[0] += 1
                        ins.then_inc(s_dve, 1)
                        dve.wait_ge(s_dve, STEPS * t + (1 + count[0]))

                    dve.wait_ge(s_adj, 16 * t + 16)
                    dve.wait_ge(s_tr, NG * t + 1)
                    link(nc.vector.tensor_scalar(E[:], s_row[:], s_min[:], None, ALU.subtract))
                    link(nc.vector.scalar_tensor_tensor(out=E[:], in0=A[:], scalar=0.0, in1=E[:],
                                                        op0=ALU.not_equal, op1=ALU.mult))
                    link(nc.vector.tensor_reduce(row_max[:, 0:1], E[:], AX.X, ALU.max))
                    link(nc.vector.tensor_scalar(row_max[:, 1:2], row_max[:, 0:1], s_min[:], S[:, t, 0:1],
                                                 ALU.add, ALU.add))
                    link(nc.vector.scalar_tensor_tensor(out=row_max[:, 2:3], in0=row_max[:, 1:2], scalar=ALPHA,
                                                        in1=row_max[:, 1:2], op0=ALU.mult, op1=ALU.max))
                    link(nc.vector.tensor_scalar(E[:], s_row[:], S[:, t, 0:1], None, ALU.add))
                    link(nc.vector.scalar_tensor_tensor(out=E[:], in0=E[:], scalar=ALPHA, in1=E[:],
                                                        op0=ALU.mult, op1=ALU.max))
                    nc.vector.tensor_scalar(E[:], E[:], row_max[:, 2:3], 1.0, ALU.subtract, ALU.min).then_inc(s_lg, 1)
                    dve.wait_ge(s_exp, t + 1)
                    nc.vector.scalar_tensor_tensor(out=E[:], in0=A[:], scalar=0.0, in1=E[:],
                                                   op0=ALU.not_equal, op1=ALU.mult).then_inc(s_pm, 1)
                    dve.wait_ge(s_mm, NG * t + NG)
                    link(nc.vector.reciprocal(den[:], ps_a[:, FOUT:FOUT + 1]))
                    nc.vector.tensor_scalar(h[:], ps_a[:, 0:FOUT], den[:], None, ALU.mult).then_inc(s_h, 1)
                    dve.wait_ge(s_g, t + 1)
                    dve.wait_ge(s_xr, 16 * t + 16)
                    link(nc.vector.tensor_tensor(y[:], y[:], xres[:], ALU.add))
                    link(nc.vector.tensor_reduce(mv[:, 0:1], y[:], AX.X, ALU.add))
                    link(nc.vector.tensor_scalar(mv[:, 0:1], mv[:, 0:1], 1.0 / FOUT, None, ALU.mult))
                    link(nc.vector.tensor_scalar(y[:], y[:], mv[:, 0:1], None, ALU.subtract))
                    link(nc.vector.tensor_tensor(h[:], y[:], y[:], ALU.mult))
                    link(nc.vector.tensor_reduce(mv[:, 1:2], h[:], AX.X, ALU.add))
                    nc.vector.tensor_scalar(mv[:, 1:2], mv[:, 1:2], 1.0 / FOUT, EPS, ALU.mult, ALU.add).then_inc(s_y, 1)
                    dve.wait_ge(s_rs, t + 1)
                    dve.wait_ge(s_st, 16 * t + 1)
                    nc.vector.tensor_scalar(o[:], y[:], rstd[:], None, ALU.mult).then_inc(s_o, 1)
                    assert count[0] == STEPS
            branch(dve, body)

        @block.tensor
        def _(pe):
            def body():
                for count in (s_xT, s_bc, s_tr,):
                    pe.sem_inc(count, 1)
                pe.wait_ge(s_w, 32)
                pe.wait_ge(s_const, 5)
                for k in range(KT):
                    for t in range(OT):
                        last = nc.tensor.transpose(ps_t[k % 2][:, bass.ts(t, P)], w_in[:, t, bass.ts(k, P)], ident[:])
                    last.then_inc(s_wT, 1)
                for k in range(KT):
                    for t in range(OT):
                        last = nc.tensor.matmul(ps_a[:, 2 * k:2 * k + 2], w_in[:, t, bass.ts(k, P)], r_in[:].rearrange("p (s t) -> p t s", t=OT)[:, t, :],
                                                start=(t == 0), stop=(t == OT - 1))
                last.then_inc(s_wr, 1)
                pe.wait_ge(s_wTc, KT)
                pe.wait_ge(s_ext, 1)
                with pe.Fori(0, NT) as t:
                    pe.wait_ge(s_x, 16 * t + 16)
                    for k in range(KT):
                        last = nc.tensor.transpose(ps_t[0][:, bass.ts(k, P)], x_in[:, bass.ts(k, P)], ident[:])
                    last.then_inc(s_xT, 1)
                    pe.wait_ge(s_xTc, t + 1)
                    pe.wait_ge(s_whc, t + 1)
                    for k in range(KT):
                        last = nc.tensor.matmul(ps_a[:, 0:FOUT + 2], xT[:, k, :], w_ext[:, k, :],
                                                start=(k == 0), stop=(k == KT - 1))
                    last.then_inc(s_wh, 1)
                with pe.Fori(0, NT) as t:
                    pe.wait_ge(s_dg, t + 1)
                    pe.wait_ge(s_row_ok, t + 1)
                    nc.tensor.matmul(ps_b[:, 0:P], ones[:], diag[:], start=True, stop=True).then_inc(s_bc, 1)
                with pe.Fori(0, NT) as t:
                    pe.wait_ge(s_pm, t + 1 + 1)
                    pe.wait_ge(s_h, t + 1)
                    for g in range(NG + 1):
                        if g < NG:
                            if g < 2:
                                pe.wait_ge(s_cp, NG * t + 1)
                            else:
                                pe.wait_ge(s_cp, NG * t + (g - 1) + 1)
                            for i in range(GRP):
                                last = nc.tensor.transpose(ps_t[g % 2][:, bass.ts(i, P)],
                                                           E[:, bass.ts(g * GRP + i, P)], ident[:])
                            last.then_inc(s_tr, 1)
                        if g > 0:
                            pe.wait_ge(s_cp, NG * t + g + 1)
                            for i in range(GRP):
                                n = (g - 1) * GRP + i
                                last = nc.tensor.matmul(ps_a[:, 0:FOUT + 1], ET[:, (g - 1) % 2, bass.ts(i, P)],
                                                        Wh[:, n, :], start=(n == 0), stop=(n == NT - 1))
                            last.then_inc(s_mm, 1)
            branch(pe, body)


def kernel(**inputs):
    import numpy as np
    import concourse.bacc as bacc
    from concourse import mybir as mb
    from concourse.bass_utils import run_bass_kernel_spmd as run

    nc = bacc.Bacc("TRN2", target_bir_lowering=False, num_devices=1)
    arrays, args = {}, []
    for name in ("x", "adj", "L0_gnn_W", "L0_gnn_r"):
        a = np.ascontiguousarray(inputs[name])
        arrays[f"in_{name}"] = a
        args.append(nc.dram_tensor(f"in_{name}", a.shape, mb.dt.from_np(a.dtype), kind="ExternalInput").ap())
    out = nc.dram_tensor("out", inputs["x"].shape, mb.dt.float32, kind="ExternalOutput").ap()
    general_path(nc, *args, out)
    got = run(nc, [arrays], core_ids=[0])
    return got.results[0]["out"]
```

```python
import concourse.bass as bass
from concourse import mybir
from contextlib import ExitStack

F32 = mybir.dt.float32
I32 = mybir.dt.int32
ALU = mybir.AluOpType
ACT = mybir.ActivationFunctionType
AX = mybir.AxisListType

P = 128
ALPHA = 0.2
EPS = 1e-5
REDUCE_MAX = bass.bass_isa.ReduceOp.max
BANK = 512


BF16 = mybir.dt.bfloat16
F32R = mybir.dt.float32r
U32 = mybir.dt.uint32

LEVEL = 60.0
MAX_SPREAD = 120.0
MAX_S = 100.0
MAX_WH = 1e6
GATE = 1e37


def narrow_path(nc, x, adj, W, r, out, w_rows, taken):
    N, FIN = x.shape
    FOUT = W.shape[0]
    NC = N // P
    NB = N // BANK
    NAH = NB // 2
    RT = BANK // P
    PC = 8
    CP = NC // PC
    GP = CP // 2
    GB = GP * PC
    KT = FIN // P
    OT = FOUT // P
    HC = FOUT + 2

    ctx = ExitStack()
    with ctx:
        def sb(name, shape, dt=F32):
            return ctx.enter_context(nc.sbuf_tensor(name, shape, dt))

        def sem(name):
            return ctx.enter_context(nc.semaphore(name))

        ident = sb("ident", [P, P])
        w_in = sb("w_in", [P, OT, FIN])
        r_in = sb("r_in", [P, 2 * OT])
        w_ext = sb("w_ext", [P, KT, FOUT + 2])
        Pw = [sb(f"Pw{i}", [P, 2, BANK]) for i in range(4)]
        x_in = Pw[2][:].rearrange("p i (r f) -> p i r f", f=FIN)
        xT = Pw[3]
        S = sb("S", [P, NC, 2])
        V = sb("V", [P, NC])
        X = sb("X", [P, NC])
        Rc = sb("Rc", [P, NC])
        Rt = sb("Rt", [NC, P])
        wh_max = sb("wh_max", [P, NC])
        red = sb("red", [P, 3])
        top = sb("top", [P, 3])
        neg_M = sb("neg_M", [P, 1])
        shift = sb("shift", [P, 1])
        fits = sb("fits", [P, 5])
        s_i_cut = sb("s_i_cut", [P, NC])
        WV_hi = sb("WV_hi", [P, NC, HC], F32R)
        WV_lo = sb("WV_lo", [P, NC, FOUT], F32R)
        adj_in = sb("adj_in", [P, 2, 16, 256], BF16)
        mask = sb("mask", [P, 4, BANK], U32)
        R_row = sb("R_row", [P, 2, BANK])
        P_hi = sb("P_hi", [P, 2, 2, BANK], F32R)
        P_lo = sb("P_lo", [P, 2, 2, BANK], F32R)
        x_res = sb("x_res", [P, RT, FIN])
        y = sb("y", [P, RT, FOUT])
        den = sb("den", [P, RT])
        rden = sb("rden", [P, RT])
        stats = sb("stats", [P, RT, 6])
        mv = sb("mv", [P, RT, 2])
        consts = sb("powers", [P, 3, RT])
        var_e = sb("var_e", [P, RT])
        rstd = sb("rstd", [P, RT])
        n_mean = sb("n_mean", [P, RT])
        bias = sb("bias", [P, RT])
        spare = sb("spare", [P, 1])
        acc = [ctx.enter_context(nc.psum_tensor(f"acc{i}", [P, RT, BANK], F32)) for i in range(2)]
        ps_xT = [acc[0][:, 0, :], acc[0][:, 1, :]]
        ps_wh = [acc[1][:, i, 0:FOUT + 2] for i in range(4)]
        mask16 = mask[:].bitcast(BF16).rearrange("p b (i r) -> p b r i", r=2)
        hi_read = P_hi[:].bitcast(F32)
        WV_hi_read = WV_hi[:].bitcast(F32)

        s_w = sem("w_loaded")
        s_const = sem("const_ready")
        s_wT = sem("w_transposed")
        s_wTc = sem("w_copied")
        s_wr = sem("w_r_product")
        s_x = [sem(f"x_loaded{i}") for i in range(2)]
        s_xT = sem("x_transposed")
        s_xTc = sem("x_copied")
        s_wh = sem("wh_product")
        s_v = sem("v_ready")
        s_hi0 = sem("wv_hi_ready")
        s_lo0 = sem("wv_lo_ready")
        s_vh = sem("v_hi_ready")
        s_vl = sem("v_lo_ready")
        s_red = sem("local_maxima")
        s_top = sem("global_maxima")
        s_dve = sem("vector_step")
        s_cut = sem("s_i_cut_ready")
        s_flag = sem("flag_ready")
        s_Rc = sem("r_columns_ready")
        s_Rt = sem("r_transposed")
        s_Rtc = sem("r_copied")
        s_Rst = sem("r_rows_stored")
        s_Rld = [sem(f"r_row_loaded{i}") for i in range(2)]
        s_adj = [sem(f"adj_loaded{i}") for i in range(2)]
        s_gate = sem("adj_gated")
        s_mask = sem("mask_transposed")
        s_p = sem("weights_ready")
        s_hi = sem("hi_ready")
        s_lo = sem("lo_ready")
        s_free = sem("group_multiplied")
        s_den = sem("denominator_ready")
        s_rden = sem("rden_ready")
        s_g = sem("gelu_done")
        s_xr = sem("xres_loaded")
        s_y = sem("y_ready")
        s_bn = sem("stats_ready")
        s_mv = sem("moments_ready")
        s_pool = sem("pool_step")
        s_bias = sem("scale_bias_ready")
        s_o = sem("out_ready")
        s_st = sem("out_stored")

        block = ctx.enter_context(nc.Block())

        x_m = x.rearrange("(a m q r) f -> m a q (r f)", a=4, m=NC // 2, q=32, r=2)
        x_t = x.rearrange("(ah u g p r) f -> ah r u g p f", ah=NAH, u=RT, g=4, p=32, r=2)
        out_t = out.rearrange("(ah u g p r) f -> ah r u g p f", ah=NAH, u=RT, g=4, p=32, r=2)
        adj_p = adj.rearrange("(ah g p r) (aj c f) -> ah r c aj p g f", ah=NAH, g=16, p=32, r=2, aj=4, c=PC)

        def applies(eng, body):
            eng.wait_ge(s_flag, 1)
            flag = eng.value_load(taken[0:1, 0:1], min_val=0, max_val=1)
            with eng.If(flag == 1):
                body()

        @block.sync
        def _(sp):
            sp.sem_inc(s_st, 1)
            sp.dma_start(w_in[:], W.rearrange("(t p) k -> p t k", p=P)).then_inc(s_w, 16)
            sp.dma_start(r_in[:], r.rearrange("(u p) a -> p (u a)", p=P),
                         allow_slow_non_contiguous=True).then_inc(s_w, 16)
            with sp.Fori(0, NC // 4) as mm:
                for i in range(2):
                    sp.wait_ge(s_xT, 2 * mm + (i + 1))
                    sp.dma_start(Pw[2][:, i, :], x_m[2 * mm + i]).then_inc(s_x[i], 16)

            def main():
                sp.wait_ge(s_Rtc, 1)
                rows = w_rows.rearrange("(a b) (g p) -> (b g) a p", a=4, p=32)
                sp.dma_start(rows, Rt[:].rearrange("k (a p) -> k a p", a=4)).then_inc(s_Rst, 16)
                sp.wait_ge(s_Rst, 16)

                def load_rows(ah, r_):
                    sp.dma_start(R_row[:, r_, :], w_rows[2 * ah + r_].partition_broadcast(P)).then_inc(s_Rld[r_], 16)

                def load_x(ah, r_):
                    for u in range(RT):
                        sp.dma_start(x_res[:, u, :], x_t[ah, r_, u]).then_inc(s_xr, 16)

                def store(ah, r_):
                    sp.wait_ge(s_o, 8 * ah + (4 * r_ + 4))
                    for u in reversed(range(RT)):
                        sp.dma_start(out_t[ah, r_, u], y[:, u, :]).then_inc(s_st, 16)

                load_rows(0, 0)
                load_rows(0, 1)
                load_x(0, 0)
                with sp.Fori(0, NAH - 1) as ah:
                    sp.wait_ge(s_p, 2 * GB * ah + GB)
                    load_rows(ah + 1, 0)
                    sp.wait_ge(s_y, 2 * ah + 1)
                    load_x(ah, 1)
                    store(ah, 0)
                    sp.wait_ge(s_p, 2 * GB * ah + 2 * GB)
                    load_rows(ah + 1, 1)
                    sp.wait_ge(s_y, 2 * ah + 2)
                    load_x(ah + 1, 0)
                    store(ah, 1)
                sp.wait_ge(s_y, NB - 1)
                load_x(NAH - 1, 1)
                store(NAH - 1, 0)
                store(NAH - 1, 1)
                sp.wait_ge(s_st, 16 * RT * NB + 1)
            applies(sp, main)

        @block.gpsimd
        def _(pool):
            def load(ah, r_, cp, i):
                for a in range(4):
                    pool.dma_start(adj_in[32 * a:32 * a + 32, i], adj_p[ah, r_, 2 * cp + i, a]).then_inc(s_adj[i], 16)

            nc.gpsimd.memset(ident[:], 0.0).then_inc(s_const, 1)
            pool.wait_ge(s_const, 1)
            nc.gpsimd.affine_select(out=ident[:], in_=ident[:], compare_op=ALU.not_equal, fill=1.0,
                                    base=0, pattern=[[-1, P]], channel_multiplier=1).then_inc(s_const, 1)
            load(0, 0, 0, 0)
            load(0, 0, 0, 1)
            for i, value in enumerate((-0.5, EPS, -1.0)):
                nc.gpsimd.memset(consts[:, i, :], value).then_inc(s_const, 1)
            pool.wait_ge(s_red, 3)
            nc.gpsimd.partition_all_reduce(top[:], red[:], P, REDUCE_MAX).then_inc(s_top, 1)

            def main():
                def residual(e):
                    pool.wait_ge(s_g, 4 * e + 12)
                    pool.wait_ge(s_xr, 16 * RT * e + 16 * RT)
                    nc.gpsimd.tensor_tensor(y[:], y[:], x_res[:], ALU.add).then_inc(s_y, 1)

                def scale_bias(e):
                    pool.wait_ge(s_mv, e + 1)
                    nc.gpsimd.tensor_tensor(var_e[:], mv[:, :, 1], consts[:, 1, :], ALU.add).then_inc(s_pool, 1)
                    nc.gpsimd.tensor_tensor(n_mean[:], mv[:, :, 0], consts[:, 2, :], ALU.mult).then_inc(s_pool, 1)
                    pool.wait_ge(s_pool, 3 * e + 2)
                    nc.gpsimd.tensor_tensor(rstd[:], var_e[:], consts[:, 0, :], ALU.pow).then_inc(s_pool, 1)
                    pool.wait_ge(s_pool, 3 * e + 3)
                    nc.gpsimd.tensor_tensor(bias[:], n_mean[:], rstd[:], ALU.mult).then_inc(s_bias, 1)

                def block_loads(ah, r_, first=0, one_before=True, two_before=True):
                    t = 2 * ah + r_
                    for c in range(first, PC):
                        pool.wait_ge(s_mask, PC * t + (c - 1))
                        load(ah, r_, c // 2, c % 2)
                        if two_before and c == 0:
                            scale_bias(t - 2)
                        if one_before and c == 4:
                            residual(t - 1)

                block_loads(0, 0, first=2, one_before=False, two_before=False)
                block_loads(0, 1, two_before=False)
                with pool.Fori(1, NAH) as ah:
                    for r_ in range(2):
                        block_loads(ah, r_)
                scale_bias(NB - 2)
                residual(NB - 1)
                scale_bias(NB - 1)
            applies(pool, main)

        @block.scalar
        def _(act):
            act.sem_inc(s_g, 2 * RT)
            for k in range(KT):
                act.wait_ge(s_wT, k + 1)
                nc.scalar.copy(w_ext[:, k, 0:FOUT], ps_xT[k % 2][:, 0:FOUT]).then_inc(s_wTc, 1)
            act.wait_ge(s_wr, 1)
            nc.scalar.copy(w_ext[:, :, FOUT:FOUT + 2],
                           acc[1][:, 0, 0:2 * KT].rearrange("p (k c) -> p k c", c=2)).then_inc(s_wTc, 1)
            with act.Fori(0, NC // 4) as mm:
                for i in range(2):
                    act.wait_ge(s_xT, 2 * mm + (i + 3))
                    nc.scalar.copy(xT[:, i, :], ps_xT[i]).then_inc(s_xTc, 1)
                for q in range(4):
                    k = 4 * mm + q
                    act.wait_ge(s_wh, k + 1)
                    nc.scalar.activation(V[:, bass.ds(k, 1)], ps_wh[q][:, FOUT + 1:FOUT + 2], ACT.Exp,
                                         scale=ALPHA).then_inc(s_v, 1)
                    act.wait_ge(s_v, k + 1)
                    nc.scalar.activation(WV_hi[:, k, 0:FOUT], ps_wh[q][:, 0:FOUT], ACT.Copy,
                                         scale=V[:, bass.ds(k, 1)]).then_inc(s_hi0, 1)
            nc.scalar.copy(WV_hi[:, :, FOUT], V[:]).then_inc(s_vh, 1)

            def gate(i, u):
                part = adj_in[:, i, 4 * u:4 * u + 4, :]
                nc.scalar.activation(part, part, ACT.Abs, scale=GATE).then_inc(s_gate, 1)

            act.wait_ge(s_adj[0], 64)
            for u in range(GP):
                gate(0, u)
            act.wait_ge(s_adj[1], 64)
            act.wait_ge(s_cut, 1)
            nc.scalar.activation(X[:], S[:, :, 1], ACT.Exp, bias=shift[:], scale=1.0 - ALPHA)
            nc.scalar.activation(Rc[:].rearrange("p (h r g) -> p h g r", h=2, r=2),
                                 s_i_cut[:].rearrange("p (h g r) -> p h g r", h=2, r=2),
                                 ACT.Exp, bias=shift[:], scale=ALPHA - 1.0).then_inc(s_Rc, 1)
            act.wait_ge(s_Rt, 1)
            nc.scalar.copy(Rt[:], acc[0][0:NC, 0, 0:P]).then_inc(s_Rtc, 1)

            def main():
                def piece(ah, r_, cp, i, ahead=True, gelu=False, norm=False):
                    t = 2 * ah + r_
                    if ahead:
                        act.wait_ge(s_adj[1 - i], 64 * (PC // 2 * t + cp) + 64 * (1 + i))
                    for u in range(GP):
                        G = GB * t + GP * (2 * cp + i) + u
                        if ahead:
                            gate(1 - i, u)
                        act.wait_ge(s_p, G + 1)
                        act.wait_ge(s_free, G + 1)
                        nc.scalar.copy(P_hi[:, u % 2], Pw[u][:]).then_inc(s_hi, 1)
                        if gelu:
                            if u == 0:
                                act.wait_ge(s_rden, t)
                                act.wait_ge(s_st, 16 * RT * (t - 1) + 1)
                            nc.scalar.activation(y[:, u, :], acc[1 - r_][:, u, 0:FOUT], ACT.Gelu,
                                                 scale=rden[:, u:u + 1]).then_inc(s_g, 1)
                        if norm:
                            if u == 0:
                                act.wait_ge(s_bias, t)
                            nc.scalar.activation(y[:, u, :], y[:, u, :], ACT.Identity, scale=rstd[:, u:u + 1],
                                                 bias=bias[:, u:u + 1]).then_inc(s_o, 1)

                def row_block(ah, r_, before=True, last=False):
                    piece(ah, r_, 0, 0)
                    piece(ah, r_, 0, 1, gelu=before)
                    with act.Fori(1, PC // 2 - 1) as cp:
                        piece(ah, r_, cp, 0)
                        piece(ah, r_, cp, 1)
                    piece(ah, r_, PC // 2 - 1, 0)
                    piece(ah, r_, PC // 2 - 1, 1, norm=before, ahead=not last)

                row_block(0, 0, before=False)
                row_block(0, 1)
                with act.Fori(1, NAH - 1) as ah:
                    for r_ in range(2):
                        row_block(ah, r_)
                row_block(NAH - 1, 0)
                row_block(NAH - 1, 1, last=True)
                act.wait_ge(s_rden, NB)
                act.wait_ge(s_st, 16 * RT * (NB - 1) + 1)
                for u in range(RT):
                    nc.scalar.activation(y[:, u, :], acc[1][:, u, 0:FOUT], ACT.Gelu,
                                         scale=rden[:, u:u + 1]).then_inc(s_g, 1)
                act.wait_ge(s_bias, NB)
                for u in range(RT):
                    nc.scalar.activation(y[:, u, :], y[:, u, :], ACT.Identity, scale=rstd[:, u:u + 1],
                                         bias=bias[:, u:u + 1]).then_inc(s_o, 1)
            applies(act, main)

        @block.vector
        def _(dve):
            dve.sem_inc(s_lo0, 4)
            with dve.Fori(0, NC // 4) as mm:
                for q in range(4):
                    k = 4 * mm + q
                    dve.wait_ge(s_hi0, k + 1)
                    nc.vector.tensor_copy(S[:, k, :], ps_wh[q][:, FOUT:FOUT + 2])
                    nc.vector.tensor_reduce(wh_max[:, bass.ds(k, 1)], ps_wh[q][:, 0:FOUT], AX.X, ALU.max,
                                            apply_absolute_value=True)
                    nc.vector.scalar_tensor_tensor(out=WV_lo[:, k, :], in0=ps_wh[q][:, 0:FOUT],
                                                   scalar=V[:, bass.ds(k, 1)],
                                                   in1=WV_hi_read[:, k, 0:FOUT],
                                                   op0=ALU.mult, op1=ALU.subtract).then_inc(s_lo0, 1)
            dve.wait_ge(s_lo0, NC + 4)
            nc.vector.tensor_reduce(red[:, 0:1], S[:, :, 1], AX.X, ALU.max).then_inc(s_red, 1)
            nc.vector.tensor_reduce(red[:, 1:2], S[:, :, 1], AX.X, ALU.min, negate=True).then_inc(s_red, 1)
            nc.vector.tensor_reduce(red[:, 2:3], wh_max[:], AX.X, ALU.max).then_inc(s_red, 1)
            dve.wait_ge(s_vh, 1)
            nc.vector.tensor_tensor(WV_hi[:, :, FOUT + 1], V[:], WV_hi_read[:, :, FOUT], ALU.subtract).then_inc(s_vl, 1)
            dve.wait_ge(s_top, 1)
            nc.vector.tensor_scalar(neg_M[:], top[:, 0:1], -1.0, None, ALU.mult).then_inc(s_dve, 1)
            nc.vector.tensor_scalar(shift[:], top[:, 0:1], -1.0, LEVEL, ALU.mult, ALU.add).then_inc(s_dve, 1)
            dve.wait_ge(s_dve, 2)
            nc.vector.tensor_scalar(s_i_cut[:], S[:, :, 0], neg_M[:], None, ALU.max).then_inc(s_cut, 1)
            nc.vector.tensor_scalar(fits[:, 0:1], top[:, 0:1], top[:, 1:2], MAX_SPREAD, ALU.add, ALU.is_le).then_inc(s_dve, 1)
            nc.vector.tensor_scalar(fits[:, 1:3], top[:, 0:2], MAX_S, None, ALU.is_le).then_inc(s_dve, 1)
            nc.vector.tensor_scalar(fits[:, 3:4], top[:, 2:3], MAX_WH, None, ALU.is_le).then_inc(s_dve, 1)
            dve.wait_ge(s_dve, 5)
            nc.vector.tensor_reduce(fits[:, 4:5], fits[:, 0:4], AX.X, ALU.min).then_inc(s_dve, 1)
            dve.wait_ge(s_dve, 6)
            nc.vector.tensor_copy(taken[0:1, 0:1], fits[0:1, 4:5]).then_inc(s_flag, 1)

            def main():
                def transpose_piece(n, i, first):
                    dve.wait_ge(s_gate, 4 * n + 4)
                    if not first:
                        dve.wait_ge(s_p, GP * n)
                    nc.vector.transpose(mask[:].rearrange("p b (g n) -> p g b n", n=32),
                                        adj_in[:, i].bitcast(U32).rearrange("p g (b n) -> p g b n", n=32)).then_inc(s_mask, 1)

                def weights(n, r_, cp, i, u, first):
                    if not first:
                        dve.wait_ge(s_lo, GP * n + (u - 3))
                    for par in range(2):
                        k = CP * (2 * cp + i) + 2 * u + par
                        last = nc.vector.scalar_tensor_tensor(out=Pw[u][:, par, :], in0=R_row[:, r_, :],
                                                              scalar=X[:, bass.ds(k, 1)], in1=mask16[:, u, par, :],
                                                              op0=ALU.max, op1=ALU.min)
                    last.then_inc(s_p, 1)

                def low_part(G, u):
                    dve.wait_ge(s_hi, G + 1)
                    dve.wait_ge(s_free, G + 1)
                    nc.vector.tensor_tensor(P_lo[:, u % 2], Pw[u][:], hi_read[:, u % 2],
                                            ALU.subtract).then_inc(s_lo, 1)

                def piece(ah, r_, cp, i, first=False, den_of=None, stats_of=None):
                    t = 2 * ah + r_
                    n = PC * t + 2 * cp + i
                    transpose_piece(n, i, first)
                    if not first:
                        low_part(GP * n - 1, GP - 1)
                    dve.wait_ge(s_mask, n + 1)
                    for u in range(GP):
                        weights(n, r_, cp, i, u, first)
                        if u > 0:
                            low_part(GP * n + (u - 1), u - 1)
                        if den_of is not None and u == 1:
                            dve.wait_ge(s_free, GB * den_of + GB + 2)
                            nc.vector.tensor_reduce(den[:], acc[1 - r_][:, :, FOUT:HC], AX.X, ALU.add).then_inc(s_den, 1)
                        if den_of is not None and u == 2:
                            dve.wait_ge(s_den, den_of + 1)
                            nc.vector.reciprocal(rden[:], den[:]).then_inc(s_rden, 1)
                        if stats_of is not None and u == 0:
                            dve.wait_ge(s_y, stats_of + 1)
                            for v in range(RT):
                                last = nc.vector.bn_stats(stats[:, v, :], y[:, v, :])
                            last.then_inc(s_bn, 1)
                        if stats_of is not None and u == 1:
                            dve.wait_ge(s_bn, stats_of + 1)
                            nc.vector.tensor_copy(spare[:], stats[:, 0, 0:1])
                            for v in range(RT):
                                last = nc.vector.bn_aggr(mv[:, v, :], stats[:, v, :])
                            last.then_inc(s_mv, 1)

                def row_block(ah, r_, before=True):
                    t = 2 * ah + r_
                    e = t - 1 if before else None
                    dve.wait_ge(s_Rld[r_], 16 * ah + 16)
                    piece(ah, r_, 0, 0, first=not before, den_of=e)
                    piece(ah, r_, 0, 1)
                    with dve.Fori(1, PC // 2 - 1) as cp:
                        piece(ah, r_, cp, 0)
                        piece(ah, r_, cp, 1)
                    piece(ah, r_, PC // 2 - 1, 0, stats_of=e)
                    piece(ah, r_, PC // 2 - 1, 1)

                row_block(0, 0, before=False)
                row_block(0, 1)
                with dve.Fori(1, NAH) as ah:
                    for r_ in range(2):
                        row_block(ah, r_)
                low_part(GB * NB - 1, GP - 1)
                dve.wait_ge(s_free, GB * NB + 2)
                nc.vector.tensor_reduce(den[:], acc[1][:, :, FOUT:HC], AX.X, ALU.add).then_inc(s_den, 1)
                dve.wait_ge(s_den, NB)
                nc.vector.reciprocal(rden[:], den[:]).then_inc(s_rden, 1)
                dve.wait_ge(s_y, NB)
                for v in range(RT):
                    last = nc.vector.bn_stats(stats[:, v, :], y[:, v, :])
                last.then_inc(s_bn, 1)
                dve.wait_ge(s_bn, NB)
                for v in range(RT):
                    last = nc.vector.bn_aggr(mv[:, v, :], stats[:, v, :])
                last.then_inc(s_mv, 1)
            applies(dve, main)

        @block.tensor
        def _(pe):
            pe.sem_inc(s_xT, 2)
            pe.sem_inc(s_free, 2)
            pe.wait_ge(s_w, 32)
            pe.wait_ge(s_const, 2)
            for k in range(KT):
                for t in range(OT):
                    last = nc.tensor.transpose(ps_xT[k % 2][:, bass.ts(t, P)], w_in[:, t, bass.ts(k, P)], ident[:])
                last.then_inc(s_wT, 1)
            for k in range(KT):
                for t in range(OT):
                    last = nc.tensor.matmul(acc[1][:, 0, 2 * k:2 * k + 2], w_in[:, t, bass.ts(k, P)],
                                            r_in[:].rearrange("p (s t) -> p t s", t=OT)[:, t, :],
                                            start=(t == 0), stop=(t == OT - 1))
            last.then_inc(s_wr, 1)
            pe.wait_ge(s_wTc, KT + 1)
            with pe.Fori(0, NC // 4) as mm:
                for i in range(2):
                    pe.wait_ge(s_x[i], 16 * mm + 16)
                    for r_ in range(2):
                        for k in range(KT):
                            last = nc.tensor.transpose(ps_xT[i][:, bass.ts(KT * r_ + k, P)],
                                                       x_in[:, i, r_, bass.ts(k, P)], ident[:])
                    last.then_inc(s_xT, 1)
                for i in range(2):
                    pe.wait_ge(s_xTc, 2 * mm + (i + 1))
                    for r_ in range(2):
                        q = 2 * i + r_
                        pe.wait_ge(s_lo0, 4 * mm + (q + 1))
                        for k in range(KT):
                            last = nc.tensor.matmul(ps_wh[q], xT[:, i, bass.ts(KT * r_ + k, P)], w_ext[:, k, :],
                                                    start=(k == 0), stop=(k == KT - 1))
                        last.then_inc(s_wh, 1)
            pe.wait_ge(s_Rc, 1)
            nc.tensor.transpose(acc[0][0:NC, 0, 0:P], Rc[:], ident[:]).then_inc(s_Rt, 1)

            def main():
                pe.wait_ge(s_vl, 1)
                pe.wait_ge(s_Rtc, 1)

                def piece(ah, r_, c, first=False, final=False):
                    for u in range(GP):
                        G = GB * (2 * ah + r_) + GP * c + u
                        pe.wait_ge(s_hi, G + 1)
                        for par in range(2):
                            k = CP * c + 2 * u + par
                            for v in range(RT):
                                nc.tensor.matmul(acc[r_][:, v, 0:HC], P_hi[:, u % 2, par, bass.ts(v, P)],
                                                 WV_hi[:, k, :], start=(first and u == 0 and par == 0),
                                                 stop=False)
                                nc.tensor.matmul(acc[r_][:, v, 0:FOUT], P_hi[:, u % 2, par, bass.ts(v, P)],
                                                 WV_lo[:, k, :], start=False, stop=False)
                        pe.wait_ge(s_lo, G + 1)
                        for par in range(2):
                            k = CP * c + 2 * u + par
                            for v in range(RT):
                                last = nc.tensor.matmul(acc[r_][:, v, 0:HC], P_lo[:, u % 2, par, bass.ts(v, P)],
                                                        WV_hi[:, k, :], start=False,
                                                        stop=(final and u == GP - 1 and par == 1))
                        last.then_inc(s_free, 1)

                with pe.Fori(0, NAH) as ah:
                    for r_ in range(2):
                        pe.wait_ge(s_g, 8 * ah + (4 * r_ + 4))
                        piece(ah, r_, 0, first=True)
                        with pe.Fori(1, PC - 1) as c:
                            piece(ah, r_, c)
                        piece(ah, r_, PC - 1, final=True)
            applies(pe, main)


def general_path(nc, x, adj, W, r, out, taken=None):
    N, FIN = x.shape
    FOUT = W.shape[0]
    NT = N // P
    KT = FIN // P
    OT = FOUT // P
    GRP = BANK // P
    NG = NT // GRP

    ctx = ExitStack()
    with ctx:
        def sb(name, shape, dt=F32):
            return ctx.enter_context(nc.sbuf_tensor("g_" + name, shape, dt))

        def pb(name, shape):
            return ctx.enter_context(nc.psum_tensor("g_" + name, shape, F32))

        def sem(name):
            return ctx.enter_context(nc.semaphore("g_" + name))

        ident = sb("ident", [P, P])
        ones = sb("ones", [P, P])
        w_in = sb("w_in", [P, OT, FIN])
        r_in = sb("r_in", [P, 2 * OT])
        w_ext = sb("w_ext", [P, KT, FOUT + 2])
        x_in = sb("x_in", [P, FIN])
        xT = sb("xT", [P, KT, P])
        Wh = sb("Wh", [P, NT, FOUT + 1])
        S = sb("S", [P, NT, 2])
        diag = sb("diag", [P, P])
        s_row = sb("s_row", [P, N])
        s_min = sb("s_min", [P, 1])
        A = sb("A", [P, N], I32)
        E = sb("E", [P, N])
        row_max = sb("row_max", [P, 3])
        ET = sb("ET", [P, 2, BANK])
        den = sb("den", [P, 1])
        xres = sb("xres", [P, FIN])
        h = sb("h", [P, FOUT])
        y = sb("y", [P, FOUT])
        o = sb("o", [P, FOUT])
        mv = sb("mv", [P, 2])
        rstd = sb("rstd", [P, 1])
        expo = sb("expo", [P, 1])
        ps_t = [pb(f"ps_t{i}", [P, BANK]) for i in range(2)]
        ps_a = pb("ps_a", [P, BANK])
        ps_b = pb("ps_b", [P, BANK])

        s_w = sem("w_loaded")
        s_const = sem("const_ready")
        s_wT = sem("w_transposed")
        s_wTc = sem("w_copied")
        s_wr = sem("w_r_product")
        s_ext = sem("w_ext_ready")
        s_x = sem("x_loaded")
        s_xT = sem("x_transposed")
        s_xTc = sem("x_copied")
        s_wh = sem("wh_product")
        s_whc = sem("wh_stored")
        s_dg = sem("diag_ready")
        s_bc = sem("row_broadcast")
        s_row_ok = sem("row_stored")
        s_dve = sem("vector_step")
        s_adj = sem("adj_loaded")
        s_lg = sem("logits_ready")
        s_exp = sem("exp_done")
        s_pm = sem("weights_masked")
        s_tr = sem("weights_transposed")
        s_cp = sem("transposed_copied")
        s_mm = sem("product_done")
        s_xr = sem("xres_loaded")
        s_h = sem("h_ready")
        s_g = sem("gelu_done")
        s_y = sem("variance_ready")
        s_rs = sem("rstd_ready")
        s_o = sem("out_ready")
        s_st = sem("out_stored")
        block = ctx.enter_context(nc.Block())

        def branch(eng, body):
            if taken is None:
                body()
            else:
                flag = eng.value_load(taken[0:1, 0:1], min_val=0, max_val=1)
                with eng.If(flag == 0):
                    body()

        @block.sync
        def _(sp):
            def body():
                for count in (s_st,):
                    sp.sem_inc(count, 1)
                sp.dma_start(w_in[:], W.rearrange("(t p) k -> p t k", p=P)).then_inc(s_w, 16)
                sp.dma_start(r_in[:], r.rearrange("(u p) a -> p (u a)", p=P),
                             allow_slow_non_contiguous=True).then_inc(s_w, 16)
                with sp.Fori(0, NT) as t:
                    sp.wait_ge(s_xT, t + 1)
                    sp.dma_start(x_in[:], x[bass.ts(t, P), :]).then_inc(s_x, 16)
                with sp.Fori(0, NT) as t:
                    sp.wait_ge(s_pm, t + 1)
                    sp.dma_start(A[:], adj[bass.ts(t, P), :]).then_inc(s_adj, 16)
                    sp.wait_ge(s_o, t + 1)
                    sp.dma_start(xres[:], x[bass.ts(t, P), :]).then_inc(s_xr, 16)
                    sp.wait_ge(s_o, t + 1 + 1)
                    sp.dma_start(out[bass.ts(t, P), :], o[:]).then_inc(s_st, 16)
                sp.wait_ge(s_st, 16 * NT + 1)
            branch(sp, body)

        @block.gpsimd
        def _(pool):
            def body():
                nc.gpsimd.memset(ident[:], 0.0).then_inc(s_const, 1)
                nc.gpsimd.memset(ones[:], 1.0).then_inc(s_const, 1)
                nc.gpsimd.memset(expo[:], -0.5).then_inc(s_const, 1)
                nc.gpsimd.memset(Wh[:, :, FOUT:FOUT + 1], 1.0).then_inc(s_const, 1)
                pool.wait_ge(s_const, 4)
                nc.gpsimd.affine_select(out=ident[:], in_=ident[:], compare_op=ALU.not_equal, fill=1.0,
                                        base=0, pattern=[[-1, P]], channel_multiplier=1).then_inc(s_const, 1)
                with pool.Fori(0, NT) as t:
                    pool.wait_ge(s_y, t + 1)
                    nc.gpsimd.tensor_tensor(rstd[:], mv[:, 1:2], expo[:], ALU.pow).then_inc(s_rs, 1)
            branch(pool, body)

        @block.scalar
        def _(act):
            def body():
                for count in (s_whc, s_row_ok, s_cp,):
                    act.sem_inc(count, 1)
                for g in range(KT):
                    act.wait_ge(s_wT, g + 1)
                    nc.scalar.copy(w_ext[:, g, 0:FOUT], ps_t[g % 2][:, 0:FOUT]).then_inc(s_wTc, 1)
                act.wait_ge(s_wr, 1)
                nc.scalar.copy(w_ext[:, :, FOUT:FOUT + 2],
                               ps_a[:, 0:2 * KT].rearrange("p (k c) -> p k c", c=2)).then_inc(s_ext, 1)
                with act.Fori(0, NT) as t:
                    act.wait_ge(s_xT, t + 1 + 1)
                    nc.scalar.copy(xT[:], ps_t[0][:, 0:FIN].rearrange("p (k m) -> p k m", m=P)).then_inc(s_xTc, 1)
                    act.wait_ge(s_wh, t + 1)
                    nc.scalar.copy(Wh[:, t, 0:FOUT], ps_a[:, 0:FOUT])
                    nc.scalar.copy(S[:, t, :], ps_a[:, FOUT:FOUT + 2]).then_inc(s_whc, 1)
                with act.Fori(0, NT) as t:
                    act.wait_ge(s_bc, t + 1 + 1)
                    nc.scalar.copy(s_row[:, bass.ts(t, P)], ps_b[:, 0:P]).then_inc(s_row_ok, 1)
                with act.Fori(0, NT) as t:
                    act.wait_ge(s_lg, t + 1)
                    nc.scalar.activation(E[:], E[:], ACT.Exp).then_inc(s_exp, 1)
                    for g in range(NG):
                        act.wait_ge(s_tr, NG * t + (g + 1) + 1)
                        if g >= 2:
                            act.wait_ge(s_mm, NG * t + (g - 1))
                        nc.scalar.copy(ET[:, g % 2, :], ps_t[g % 2][:]).then_inc(s_cp, 1)
                    act.wait_ge(s_h, t + 1 + 1)
                    nc.scalar.activation(y[:], h[:], ACT.Gelu).then_inc(s_g, 1)
            branch(act, body)

        @block.vector
        def _(dve):
            def body():
                for count in (s_pm, s_h, s_o,):
                    dve.sem_inc(count, 1)
                with dve.Fori(0, NT) as t:
                    dve.wait_ge(s_const, 5)
                    dve.wait_ge(s_whc, NT + 1)
                    dve.wait_ge(s_bc, t + 1)
                    nc.vector.tensor_scalar(diag[:], ident[:], S[:, t, 1:2], None, ALU.mult).then_inc(s_dg, 1)
                dve.wait_ge(s_row_ok, NT + 1)
                nc.vector.tensor_reduce(s_min[:], s_row[:], AX.X, ALU.min).then_inc(s_dve, 1)
                dve.wait_ge(s_dve, 1)
                with dve.Fori(0, NT) as t:
                    STEPS = 14
                    count = [0]

                    def link(ins):
                        count[0] += 1
                        ins.then_inc(s_dve, 1)
                        dve.wait_ge(s_dve, STEPS * t + (1 + count[0]))

                    dve.wait_ge(s_adj, 16 * t + 16)
                    dve.wait_ge(s_tr, NG * t + 1)
                    link(nc.vector.tensor_scalar(E[:], s_row[:], s_min[:], None, ALU.subtract))
                    link(nc.vector.scalar_tensor_tensor(out=E[:], in0=A[:], scalar=0.0, in1=E[:],
                                                        op0=ALU.not_equal, op1=ALU.mult))
                    link(nc.vector.tensor_reduce(row_max[:, 0:1], E[:], AX.X, ALU.max))
                    link(nc.vector.tensor_scalar(row_max[:, 1:2], row_max[:, 0:1], s_min[:], S[:, t, 0:1],
                                                 ALU.add, ALU.add))
                    link(nc.vector.scalar_tensor_tensor(out=row_max[:, 2:3], in0=row_max[:, 1:2], scalar=ALPHA,
                                                        in1=row_max[:, 1:2], op0=ALU.mult, op1=ALU.max))
                    link(nc.vector.tensor_scalar(E[:], s_row[:], S[:, t, 0:1], None, ALU.add))
                    link(nc.vector.scalar_tensor_tensor(out=E[:], in0=E[:], scalar=ALPHA, in1=E[:],
                                                        op0=ALU.mult, op1=ALU.max))
                    nc.vector.tensor_scalar(E[:], E[:], row_max[:, 2:3], 1.0, ALU.subtract, ALU.min).then_inc(s_lg, 1)
                    dve.wait_ge(s_exp, t + 1)
                    nc.vector.scalar_tensor_tensor(out=E[:], in0=A[:], scalar=0.0, in1=E[:],
                                                   op0=ALU.not_equal, op1=ALU.mult).then_inc(s_pm, 1)
                    dve.wait_ge(s_mm, NG * t + NG)
                    link(nc.vector.reciprocal(den[:], ps_a[:, FOUT:FOUT + 1]))
                    nc.vector.tensor_scalar(h[:], ps_a[:, 0:FOUT], den[:], None, ALU.mult).then_inc(s_h, 1)
                    dve.wait_ge(s_g, t + 1)
                    dve.wait_ge(s_xr, 16 * t + 16)
                    link(nc.vector.tensor_tensor(y[:], y[:], xres[:], ALU.add))
                    link(nc.vector.tensor_reduce(mv[:, 0:1], y[:], AX.X, ALU.add))
                    link(nc.vector.tensor_scalar(mv[:, 0:1], mv[:, 0:1], 1.0 / FOUT, None, ALU.mult))
                    link(nc.vector.tensor_scalar(y[:], y[:], mv[:, 0:1], None, ALU.subtract))
                    link(nc.vector.tensor_tensor(h[:], y[:], y[:], ALU.mult))
                    link(nc.vector.tensor_reduce(mv[:, 1:2], h[:], AX.X, ALU.add))
                    nc.vector.tensor_scalar(mv[:, 1:2], mv[:, 1:2], 1.0 / FOUT, EPS, ALU.mult, ALU.add).then_inc(s_y, 1)
                    dve.wait_ge(s_rs, t + 1)
                    dve.wait_ge(s_st, 16 * t + 1)
                    nc.vector.tensor_scalar(o[:], y[:], rstd[:], None, ALU.mult).then_inc(s_o, 1)
                    assert count[0] == STEPS
            branch(dve, body)

        @block.tensor
        def _(pe):
            def body():
                for count in (s_xT, s_bc, s_tr,):
                    pe.sem_inc(count, 1)
                pe.wait_ge(s_w, 32)
                pe.wait_ge(s_const, 5)
                for k in range(KT):
                    for t in range(OT):
                        last = nc.tensor.transpose(ps_t[k % 2][:, bass.ts(t, P)], w_in[:, t, bass.ts(k, P)], ident[:])
                    last.then_inc(s_wT, 1)
                for k in range(KT):
                    for t in range(OT):
                        last = nc.tensor.matmul(ps_a[:, 2 * k:2 * k + 2], w_in[:, t, bass.ts(k, P)], r_in[:].rearrange("p (s t) -> p t s", t=OT)[:, t, :],
                                                start=(t == 0), stop=(t == OT - 1))
                last.then_inc(s_wr, 1)
                pe.wait_ge(s_wTc, KT)
                pe.wait_ge(s_ext, 1)
                with pe.Fori(0, NT) as t:
                    pe.wait_ge(s_x, 16 * t + 16)
                    for k in range(KT):
                        last = nc.tensor.transpose(ps_t[0][:, bass.ts(k, P)], x_in[:, bass.ts(k, P)], ident[:])
                    last.then_inc(s_xT, 1)
                    pe.wait_ge(s_xTc, t + 1)
                    pe.wait_ge(s_whc, t + 1)
                    for k in range(KT):
                        last = nc.tensor.matmul(ps_a[:, 0:FOUT + 2], xT[:, k, :], w_ext[:, k, :],
                                                start=(k == 0), stop=(k == KT - 1))
                    last.then_inc(s_wh, 1)
                with pe.Fori(0, NT) as t:
                    pe.wait_ge(s_dg, t + 1)
                    pe.wait_ge(s_row_ok, t + 1)
                    nc.tensor.matmul(ps_b[:, 0:P], ones[:], diag[:], start=True, stop=True).then_inc(s_bc, 1)
                with pe.Fori(0, NT) as t:
                    pe.wait_ge(s_pm, t + 1 + 1)
                    pe.wait_ge(s_h, t + 1)
                    for g in range(NG + 1):
                        if g < NG:
                            if g < 2:
                                pe.wait_ge(s_cp, NG * t + 1)
                            else:
                                pe.wait_ge(s_cp, NG * t + (g - 1) + 1)
                            for i in range(GRP):
                                last = nc.tensor.transpose(ps_t[g % 2][:, bass.ts(i, P)],
                                                           E[:, bass.ts(g * GRP + i, P)], ident[:])
                            last.then_inc(s_tr, 1)
                        if g > 0:
                            pe.wait_ge(s_cp, NG * t + g + 1)
                            for i in range(GRP):
                                n = (g - 1) * GRP + i
                                last = nc.tensor.matmul(ps_a[:, 0:FOUT + 1], ET[:, (g - 1) % 2, bass.ts(i, P)],
                                                        Wh[:, n, :], start=(n == 0), stop=(n == NT - 1))
                            last.then_inc(s_mm, 1)
            branch(pe, body)


def layer(nc, x, adj, W, r, out):
    w_rows = nc.dram_tensor("w_rows", (x.shape[0] // BANK, BANK), F32).ap()
    with nc.sbuf_tensor("taken", [1, 1], I32) as taken:
        narrow_path(nc, x, adj, W, r, out, w_rows, taken)
        general_path(nc, x, adj, W, r, out, taken)


def kernel(**inputs):
    import numpy as np
    import concourse.bacc as bacc
    from concourse import mybir as mb
    from concourse.bass_utils import run_bass_kernel_spmd as run

    nc = bacc.Bacc("TRN2", target_bir_lowering=False, num_devices=1)
    arrays, args = {}, []
    for name in ("x", "adj", "L0_gnn_W", "L0_gnn_r"):
        a = np.ascontiguousarray(inputs[name])
        arrays[f"in_{name}"] = a
        args.append(nc.dram_tensor(f"in_{name}", a.shape, mb.dt.from_np(a.dtype), kind="ExternalInput").ap())
    out = nc.dram_tensor("out", inputs["x"].shape, mb.dt.float32, kind="ExternalOutput").ap()
    layer(nc, *args, out)
    got = run(nc, [arrays], core_ids=[0])
    return got.results[0]["out"]
```

```python
import concourse.bass as bass
from concourse import mybir
from contextlib import ExitStack

F32 = mybir.dt.float32
I32 = mybir.dt.int32
ALU = mybir.AluOpType
ACT = mybir.ActivationFunctionType
AX = mybir.AxisListType

P = 128
ALPHA = 0.2
EPS = 1e-5
REDUCE_MAX = bass.bass_isa.ReduceOp.max
BANK = 512


BF16 = mybir.dt.bfloat16
U8 = mybir.dt.uint8
F32R = mybir.dt.float32r
U32 = mybir.dt.uint32

LEVEL = 54.0
MAX_SPREAD = 120.0
MAX_S = 100.0
MAX_WH = 1e6
GATE = 255.0


def narrow_path(nc, x, adj, W, r, out, w_rows, taken):
    N, FIN = x.shape
    FOUT = W.shape[0]
    NC = N // P
    NB = N // BANK
    NAH = NB // 2
    RT = BANK // P
    PC = 8
    CP = NC // PC
    GP = CP // 2
    GB = GP * PC
    KT = FIN // P
    OT = FOUT // P
    HC = FOUT + 2

    ctx = ExitStack()
    with ctx:
        def sb(name, shape, dt=F32):
            return ctx.enter_context(nc.sbuf_tensor(name, shape, dt))

        def sem(name):
            return ctx.enter_context(nc.semaphore(name))

        ident = sb("ident", [P, P])
        w_in = sb("w_in", [P, OT, FIN])
        r_in = sb("r_in", [P, 2 * OT])
        w_ext = sb("w_ext", [P, KT, FOUT + 2])
        Pw = [sb(f"Pw{i}", [P, 2, BANK]) for i in range(4)]
        x_in = [Pw[1 + b // 2][:, b % 2, :] for b in range(4)]
        xT = Pw[3]
        S = sb("S", [P, NC, 2])
        V = sb("V", [P, NC])
        X = sb("X", [P, NC])
        Rc = sb("Rc", [P, NC])
        Rt = w_in[0:NC, 0, 0:P]
        wh_max = sb("wh_max", [P, NC])
        red = sb("red", [P, 3])
        top = sb("top", [P, 3])
        neg_M = sb("neg_M", [P, 1])
        shift = sb("shift", [P, 1])
        fits = sb("fits", [P, 5])
        s_i_cut = sb("s_i_cut", [P, NC])
        WV_hi = sb("WV_hi", [P, NC, HC], F32R)
        WV_lo = sb("WV_lo", [P, NC, FOUT], F32R)
        adj_in = sb("adj_in", [P, 2, 16, 256], BF16)
        gates = sb("gates", [P, 2, 16, 256], U8)
        gatesT = sb("gatesT", [P, 2, BANK], U32)
        R_row = sb("R_row", [P, 2, BANK])
        P_hi = sb("P_hi", [P, 2, 2, BANK], F32R)
        P_lo = sb("P_lo", [P, 2, 2, BANK], F32R)
        x_res = sb("x_res", [P, RT, FIN])
        y = sb("y", [P, RT, FOUT])
        den = sb("den", [P, RT])
        rden = sb("rden", [P, RT])
        consts = sb("consts", [P, 4, RT])
        sums = sb("sums", [P, RT])
        squares = sb("squares", [P, RT])
        var = sb("var", [P, RT])
        stats = sb("stats", [P, RT, 6])
        moments = sb("moments", [P, RT, 2])
        var_e = sb("var_e", [P, RT])
        rstd = sb("rstd", [P, RT])
        n_mean = sb("n_mean", [P, RT])
        bias = sb("bias", [P, RT])
        acc = [ctx.enter_context(nc.psum_tensor(f"acc{i}", [P, RT, BANK], F32)) for i in range(2)]
        ps_xT = [acc[0][:, 0, :], acc[0][:, 1, :]]
        ps_wh = [acc[1][:, 2 * i:2 * i + 2, 0:FOUT + 2] for i in range(2)]
        gate_of = gatesT[:].bitcast(U8).rearrange("p b (i r) -> p b r i", r=4)
        hi_read = P_hi[:].bitcast(F32)
        WV_hi_read = WV_hi[:].bitcast(F32)

        s_w = sem("w_loaded")
        s_const = sem("const_ready")
        s_wT = sem("w_transposed")
        s_wTc = sem("w_copied")
        s_wr = sem("w_r_product")
        s_x = [sem(f"x_loaded{b}") for b in range(4)]
        s_xT = sem("x_transposed")
        s_xTc = sem("x_copied")
        s_wh = sem("wh_product")
        s_v = sem("v_ready")
        s_hi0 = sem("wv_hi_ready")
        s_lo0 = sem("wv_lo_ready")
        s_vh = sem("v_hi_ready")
        s_vl = sem("v_lo_ready")
        s_s = sem("s_copied")
        s_red = sem("local_maxima")
        s_top = sem("global_maxima")
        s_dve = sem("vector_step")
        s_cut = sem("s_i_cut_ready")
        s_flag = sem("flag_ready")
        s_Rc = sem("r_columns_ready")
        s_Rt = sem("r_transposed")
        s_Rtc = sem("r_copied")
        s_Rst = sem("r_rows_stored")
        s_Rld = [sem(f"r_row_loaded{i}") for i in range(2)]
        s_adj = [sem(f"adj_loaded{i}") for i in range(2)]
        s_gate = sem("adj_gated")
        s_mask = sem("gates_transposed")
        s_p = sem("weights_ready")
        s_hi = sem("hi_ready")
        s_lo = sem("lo_ready")
        s_free = sem("group_multiplied")
        s_den = sem("denominator_ready")
        s_rden = sem("rden_ready")
        s_g = sem("gelu_done")
        s_xr = sem("xres_loaded")
        s_y = sem("y_ready")
        s_sum = sem("row_sums_ready")
        s_mean = sem("mean_ready")
        s_sq = sem("row_squares_ready")
        s_pool = sem("pool_step")
        s_bias = sem("scale_bias_ready")
        s_lasty = sem("last_y_ready")
        s_lastbn = sem("last_stats_ready")
        s_lastmv = sem("last_moments_ready")
        s_lastvar = sem("last_variances_ready")
        s_lastrs = sem("last_rstd_ready")
        s_lasto = sem("last_out_ready")
        s_o = sem("out_ready")
        s_st = sem("out_stored")

        block = ctx.enter_context(nc.Block())

        x_m = x.rearrange("(a m c q s r) f -> m c s a q (r f)", a=4, m=NC // 8, c=2, q=32, s=2, r=2)
        x_t = x.rearrange("(a u g p s r) f -> a s r u g p f", a=4, u=RT, g=4, p=32, s=2, r=2)
        out_t = out.rearrange("(a u g p s r) f -> a s r u g p f", a=4, u=RT, g=4, p=32, s=2, r=2)
        adj_p = adj.rearrange("(a g p s r) (aj c f) -> a s r c aj p g f", a=4, g=16, p=32, s=2, r=2, aj=4, c=PC)

        def applies(eng, body):
            eng.wait_ge(s_flag, 1)
            flag = eng.value_load(taken[0:1, 0:1], min_val=0, max_val=1)
            with eng.If(flag == 1):
                body()

        @block.sync
        def _(sp):
            sp.sem_inc(s_st, 1)
            sp.dma_start(w_in[:], W.rearrange("(t p) k -> p t k", p=P)).then_inc(s_w, 16)
            sp.dma_start(r_in[:], r.rearrange("(u p) a -> p (u a)", p=P),
                         allow_slow_non_contiguous=True).then_inc(s_w, 16)
            with sp.Fori(0, NC // 8) as m:
                for b in range(4):
                    sp.wait_ge(s_xT, 4 * m + (b + 1))
                    sp.dma_start(x_in[b], x_m[m, b // 2, b % 2]).then_inc(s_x[b], 16)

            sp.wait_ge(s_Rtc, 1)
            rows = w_rows.rearrange("(a b) (g p) -> (b g) a p", a=4, p=32)
            sp.dma_start(rows, Rt.rearrange("k (a p) -> k a p", a=4)).then_inc(s_Rst, 16)
            sp.wait_ge(s_Rst, 16)

            def load_rows(ah, r_):
                sp.dma_start(R_row[:, r_, :], w_rows[2 * ah + r_].partition_broadcast(P)).then_inc(s_Rld[r_], 16)

            load_rows(0, 0)
            sp.wait_ge(s_Rld[0], 16)

            def main():
                def load_x(ah, r_):
                    for u in range(RT):
                        sp.dma_start(x_res[:, u, :], x_t[ah // 2, ah % 2, r_, u]).then_inc(s_xr, 16)

                def store(ah, r_):
                    sp.wait_ge(s_o, 8 * ah + (4 * r_ + 4))
                    for u in reversed(range(RT)):
                        sp.dma_start(out_t[ah // 2, ah % 2, r_, u], y[:, u, :]).then_inc(s_st, 16)

                load_rows(0, 1)
                load_x(0, 0)
                with sp.Fori(0, NAH - 1) as ah:
                    sp.wait_ge(s_p, 2 * GB * ah + GB)
                    load_rows(ah + 1, 0)
                    sp.wait_ge(s_sq, 2 * RT * ah + RT)
                    load_x(ah, 1)
                    store(ah, 0)
                    sp.wait_ge(s_p, 2 * GB * ah + 2 * GB)
                    load_rows(ah + 1, 1)
                    sp.wait_ge(s_sq, 2 * RT * ah + 2 * RT)
                    load_x(ah + 1, 0)
                    store(ah, 1)
                sp.wait_ge(s_sq, RT * (NB - 1))
                load_x(NAH - 1, 1)
                store(NAH - 1, 0)
                for u in range(RT):
                    if u < RT // 2:
                        sp.wait_ge(s_o, RT * (NB - 1) + u + 1)
                    else:
                        sp.wait_ge(s_lasto, u - RT // 2 + 1)
                    sp.dma_start(out_t[(NAH - 1) // 2, (NAH - 1) % 2, 1, u], y[:, u, :]).then_inc(s_st, 16)
                sp.wait_ge(s_st, 16 * RT * NB + 1)
            applies(sp, main)

        def two_on(m, b):
            return (m, b + 2) if b < 2 else (m + 1, b - 2)

        @block.gpsimd
        def _(pool):
            def load(ah, r_, cp, i):
                for a in range(4):
                    pool.dma_start(adj_in[32 * a:32 * a + 32, i], adj_p[ah // 2, ah % 2, r_, 2 * cp + i, a]).then_inc(s_adj[i], 16)

            nc.gpsimd.memset(ident[:], 0.0).then_inc(s_const, 1)
            pool.wait_ge(s_const, 1)
            nc.gpsimd.affine_select(out=ident[:], in_=ident[:], compare_op=ALU.not_equal, fill=1.0,
                                    base=0, pattern=[[-1, P]], channel_multiplier=1).then_inc(s_const, 1)
            load(0, 0, 0, 0)
            load(0, 0, 0, 1)
            for i, value in enumerate((-0.5, EPS, -1.0 / FOUT, 1.0 / FOUT)):
                nc.gpsimd.memset(consts[:, i, :], value).then_inc(s_const, 1)
            pool.wait_ge(s_red, 2)
            nc.gpsimd.partition_all_reduce(top[:, 0:2], red[:, 0:2], P, REDUCE_MAX).then_inc(s_top, 1)
            pool.wait_ge(s_red, 3)
            nc.gpsimd.partition_all_reduce(top[:, 2:3], red[:, 2:3], P, REDUCE_MAX).then_inc(s_top, 1)

            def main():
                def residual(e):
                    pool.wait_ge(s_g, 4 * e + 12)
                    pool.wait_ge(s_xr, 16 * RT * e + 16 * RT)
                    nc.gpsimd.tensor_tensor(y[:], y[:], x_res[:], ALU.add).then_inc(s_y, 1)

                def mean(e):
                    pool.wait_ge(s_sum, RT * e + RT)
                    nc.gpsimd.tensor_tensor(n_mean[:], sums[:], consts[:, 2, :], ALU.mult).then_inc(s_mean, 1)

                def scale_bias(e):
                    pool.wait_ge(s_sq, RT * e + RT)
                    nc.gpsimd.tensor_tensor(var[:], squares[:], consts[:, 3, :], ALU.mult).then_inc(s_pool, 1)
                    pool.wait_ge(s_pool, 3 * e + 1)
                    nc.gpsimd.tensor_tensor(var_e[:], var[:], consts[:, 1, :], ALU.add).then_inc(s_pool, 1)
                    pool.wait_ge(s_pool, 3 * e + 2)
                    nc.gpsimd.tensor_tensor(rstd[:], var_e[:], consts[:, 0, :], ALU.pow).then_inc(s_pool, 1)
                    pool.wait_ge(s_pool, 3 * e + 3)
                    nc.gpsimd.tensor_tensor(bias[:], n_mean[:], rstd[:], ALU.mult).then_inc(s_bias, 1)

                def block_loads(ah, r_, first=0, before=True):
                    t = 2 * ah + r_
                    for c in range(first, PC):
                        pool.wait_ge(s_gate, GP * PC * t + GP * (c - 1))
                        load(ah, r_, c // 2, c % 2)
                        if before and c == 4:
                            residual(t - 1)
                        if before and c == 6:
                            mean(t - 1)
                        if before and c == 7:
                            scale_bias(t - 1)

                block_loads(0, 0, first=2, before=False)
                block_loads(0, 1)
                with pool.Fori(1, NAH) as ah:
                    for r_ in range(2):
                        block_loads(ah, r_)
                pool.wait_ge(s_lastvar, 1)
                nc.gpsimd.tensor_tensor(rstd[:], var_e[:], consts[:, 0, :], ALU.pow).then_inc(s_lastrs, 1)
            applies(pool, main)

        @block.scalar
        def _(act):
            act.sem_inc(s_g, 2 * RT)
            for k in range(KT):
                act.wait_ge(s_wT, k + 1)
                nc.scalar.copy(w_ext[:, k, 0:FOUT], ps_xT[k % 2][:, 0:FOUT]).then_inc(s_wTc, 1)
            act.wait_ge(s_wr, 1)
            nc.scalar.copy(w_ext[:, :, FOUT:FOUT + 2],
                           acc[1][:, 0, 0:2 * KT].rearrange("p (k c) -> p k c", c=2)).then_inc(s_wTc, 1)

            def copy_x(m, b):
                act.wait_ge(s_xT, 4 * m + (b + 5))
                nc.scalar.copy(xT[:, b % 2, :], ps_xT[b % 2]).then_inc(s_xTc, 1)

            def high_part(m, b):
                act.wait_ge(s_wh, 4 * m + (b + 1))
                nc.scalar.activation(V[:, bass.ds(8 * m + 2 * b, 2)], ps_wh[b % 2][:, :, FOUT + 1], ACT.Exp,
                                     scale=ALPHA).then_inc(s_v, 1)
                act.wait_ge(s_v, 4 * m + (b + 1))
                for r_ in range(2):
                    k = 8 * m + (2 * b + r_)
                    nc.scalar.activation(WV_hi[:, k, 0:FOUT], ps_wh[b % 2][:, r_, 0:FOUT], ACT.Copy,
                                         scale=V[:, bass.ds(k, 1)]).then_inc(s_hi0, 1)

            copy_x(0, 0)
            copy_x(0, 1)
            with act.Fori(0, NC // 8 - 1) as m:
                for b in range(4):
                    high_part(m, b)
                    copy_x(*two_on(m, b))

            def gate(i, u):
                nc.scalar.activation(gates[:, i, 4 * u:4 * u + 4, :], adj_in[:, i, 4 * u:4 * u + 4, :], ACT.Abs,
                                     scale=GATE).then_inc(s_gate, 1)

            act.wait_ge(s_adj[0], 64)
            for b in range(4):
                high_part(NC // 8 - 1, b)
                if b < 2:
                    copy_x(NC // 8 - 1, b + 2)
                if b > 0:
                    gate(0, b - 1)
            nc.scalar.copy(WV_hi[:, :, FOUT], V[:]).then_inc(s_vh, 1)

            gate(0, GP - 1)
            act.wait_ge(s_adj[1], 64)
            act.wait_ge(s_cut, 1)
            nc.scalar.activation(Rc[:].rearrange("p (r m) -> p m r", r=4),
                                 s_i_cut[:].rearrange("p (m r) -> p m r", r=4),
                                 ACT.Exp, bias=shift[:], scale=ALPHA - 1.0).then_inc(s_Rc, 1)
            nc.scalar.activation(X[:], S[:, :, 1], ACT.Exp, bias=shift[:], scale=1.0 - ALPHA)
            act.wait_ge(s_Rt, 1)
            nc.scalar.copy(Rt, acc[0][0:NC, 0, 0:P]).then_inc(s_Rtc, 1)

            def main():
                def gelu(e, r_, u):
                    if u == 0:
                        act.wait_ge(s_rden, e + 1)
                        act.wait_ge(s_st, 16 * RT * e + 1)
                    nc.scalar.activation(y[:, u, :], acc[r_][:, u, 0:FOUT], ACT.Gelu,
                                         scale=rden[:, u:u + 1]).then_inc(s_g, 1)

                def row_sums(e, r_, u):
                    if u == 0:
                        act.wait_ge(s_y, e + 1)
                    nc.scalar.activation(x_res[:, u, :], y[:, u, :], ACT.Identity,
                                         accum_out=sums[:, u:u + 1]).then_inc(s_sum, 1)

                def row_squares(e, r_, u):
                    if u == 0:
                        act.wait_ge(s_mean, e + 1)
                    nc.scalar.activation(x_res[:, u, :], y[:, u, :], ACT.Square, bias=n_mean[:, u:u + 1],
                                         accum_out=squares[:, u:u + 1]).then_inc(s_sq, 1)

                def scaled(e, r_, u):
                    if u == 0:
                        act.wait_ge(s_bias, e + 1)
                    nc.scalar.activation(y[:, u, :], y[:, u, :], ACT.Identity, scale=rstd[:, u:u + 1],
                                         bias=bias[:, u:u + 1]).then_inc(s_o, 1)

                steps = {1: gelu, 3: row_sums, 5: row_squares, 7: scaled}

                def row_block(ah, r_, before=True, last=False):
                    t = 2 * ah + r_
                    for c in range(PC):
                        ahead = not (last and c == PC - 1)
                        if ahead:
                            act.wait_ge(s_adj[1 - c % 2], 64 * (PC // 2 * t + c // 2) + 64 * (1 + c % 2))
                            if before or c > 0:
                                act.wait_ge(s_mask, PC * t + c)
                        for u in range(GP):
                            G = GB * t + GP * c + u
                            if ahead:
                                gate(1 - c % 2, u)
                            act.wait_ge(s_p, G + 1)
                            act.wait_ge(s_free, G + 1)
                            nc.scalar.copy(P_hi[:, u % 2], Pw[u][:]).then_inc(s_hi, 1)
                            if before and c in steps:
                                steps[c](t - 1, 1 - r_, u)

                row_block(0, 0, before=False)
                row_block(0, 1)
                with act.Fori(1, NAH - 1) as ah:
                    for r_ in range(2):
                        row_block(ah, r_)
                row_block(NAH - 1, 0)
                row_block(NAH - 1, 1, last=True)
                for u in range(RT):
                    gelu(NB - 1, 1, u)
                for u in range(RT // 2):
                    scaled(NB - 1, 1, u)
            applies(act, main)

        @block.vector
        def _(dve):
            def transpose_piece(n, i):
                dve.wait_ge(s_gate, GP * n + GP)
                nc.vector.transpose(gatesT[:].rearrange("p b (g n) -> p g b n", n=32),
                                    gates[:, i].bitcast(U32).rearrange("p g (b n) -> p g b n", n=32)).then_inc(s_mask, 1)

            dve.sem_inc(s_lo0, 4)

            def copy_s(k, q):
                dve.wait_ge(s_hi0, k + 1)
                nc.vector.tensor_copy(S[:, k, :], ps_wh[q // 2][:, q % 2, FOUT:FOUT + 2]).then_inc(s_s, 1)

            def wh_maximum(k, q):
                nc.vector.tensor_reduce(wh_max[:, bass.ds(k, 1)], ps_wh[q // 2][:, q % 2, 0:FOUT], AX.X, ALU.max,
                                        apply_absolute_value=True)

            def low_part_wh(k, q):
                nc.vector.scalar_tensor_tensor(out=WV_lo[:, k, :], in0=ps_wh[q // 2][:, q % 2, 0:FOUT],
                                               scalar=V[:, bass.ds(k, 1)], in1=WV_hi_read[:, k, 0:FOUT],
                                               op0=ALU.mult, op1=ALU.subtract).then_inc(s_lo0, 1)

            with dve.Fori(0, NC // 4 - 1) as m:
                for q in range(4):
                    copy_s(4 * m + q, q)
                    wh_maximum(4 * m + q, q)
                    low_part_wh(4 * m + q, q)
            for q in range(2):
                copy_s(NC - 4 + q, q)
                wh_maximum(NC - 4 + q, q)
                low_part_wh(NC - 4 + q, q)
            for q in range(2, 4):
                copy_s(NC - 4 + q, q)
            dve.wait_ge(s_s, NC)
            nc.vector.tensor_reduce(red[:, 0:1], S[:, :, 1], AX.X, ALU.max).then_inc(s_red, 1)
            nc.vector.tensor_reduce(red[:, 1:2], S[:, :, 1], AX.X, ALU.min, negate=True).then_inc(s_red, 1)
            dve.wait_ge(s_top, 1)
            nc.vector.tensor_scalar(neg_M[:], top[:, 0:1], -1.0, None, ALU.mult).then_inc(s_dve, 1)
            nc.vector.tensor_scalar(shift[:], top[:, 0:1], -1.0, LEVEL, ALU.mult, ALU.add).then_inc(s_dve, 1)
            dve.wait_ge(s_dve, 2)
            nc.vector.tensor_scalar(s_i_cut[:], S[:, :, 0], neg_M[:], None, ALU.max).then_inc(s_cut, 1)
            for q in range(2, 4):
                wh_maximum(NC - 4 + q, q)
                low_part_wh(NC - 4 + q, q)
            dve.wait_ge(s_lo0, NC + 4)
            nc.vector.tensor_reduce(red[:, 2:3], wh_max[:], AX.X, ALU.max).then_inc(s_red, 1)
            dve.wait_ge(s_vh, 1)
            nc.vector.tensor_tensor(WV_hi[:, :, FOUT + 1], V[:], WV_hi_read[:, :, FOUT], ALU.subtract).then_inc(s_vl, 1)
            dve.wait_ge(s_top, 2)
            nc.vector.tensor_scalar(fits[:, 0:1], top[:, 0:1], top[:, 1:2], MAX_SPREAD, ALU.add, ALU.is_le).then_inc(s_dve, 1)
            nc.vector.tensor_scalar(fits[:, 1:3], top[:, 0:2], MAX_S, None, ALU.is_le).then_inc(s_dve, 1)
            nc.vector.tensor_scalar(fits[:, 3:4], top[:, 2:3], MAX_WH, None, ALU.is_le).then_inc(s_dve, 1)
            dve.wait_ge(s_dve, 5)
            nc.vector.tensor_reduce(fits[:, 4:5], fits[:, 0:4], AX.X, ALU.min).then_inc(s_dve, 1)
            dve.wait_ge(s_dve, 6)
            nc.vector.tensor_copy(taken[0:1, 0:1], fits[0:1, 4:5]).then_inc(s_flag, 1)

            transpose_piece(0, 0)

            def main():
                def weights(n, r_, cp, i, u, first):
                    if not first:
                        dve.wait_ge(s_lo, GP * n + (u - 3))
                    for par in range(2):
                        k = CP * (2 * cp + i) + 2 * u + par
                        last = nc.vector.scalar_tensor_tensor(out=Pw[u][:, par, :], in0=R_row[:, r_, :],
                                                              scalar=X[:, bass.ds(k, 1)], in1=gate_of[:, u // 2, 2 * (u % 2) + par, :],
                                                              op0=ALU.max, op1=ALU.mult)
                    last.then_inc(s_p, 1)

                def low_part(G, u):
                    dve.wait_ge(s_hi, G + 1)
                    dve.wait_ge(s_free, G + 1)
                    nc.vector.tensor_tensor(P_lo[:, u % 2], Pw[u][:], hi_read[:, u % 2],
                                            ALU.subtract).then_inc(s_lo, 1)

                def piece(ah, r_, cp, i, first=False, den_of=None):
                    t = 2 * ah + r_
                    n = PC * t + 2 * cp + i
                    if not first:
                        dve.wait_ge(s_p, GP * n)
                        transpose_piece(n, i)
                        low_part(GP * n - 1, GP - 1)
                    dve.wait_ge(s_mask, n + 1)
                    for u in range(GP):
                        weights(n, r_, cp, i, u, first)
                        if u > 0:
                            low_part(GP * n + (u - 1), u - 1)
                        if den_of is not None and u == 1:
                            dve.wait_ge(s_free, GB * den_of + GB + 2)
                            nc.vector.tensor_reduce(den[:], acc[1 - r_][:, :, FOUT:HC], AX.X, ALU.add).then_inc(s_den, 1)
                        if den_of is not None and u == 2:
                            dve.wait_ge(s_den, den_of + 1)
                            nc.vector.reciprocal(rden[:], den[:]).then_inc(s_rden, 1)

                def row_block(ah, r_, before=True):
                    t = 2 * ah + r_
                    e = t - 1 if before else None
                    dve.wait_ge(s_Rld[r_], 16 * ah + 16)
                    piece(ah, r_, 0, 0, first=not before, den_of=e)
                    piece(ah, r_, 0, 1)
                    with dve.Fori(1, PC // 2) as cp:
                        piece(ah, r_, cp, 0)
                        piece(ah, r_, cp, 1)

                row_block(0, 0, before=False)
                row_block(0, 1)
                with dve.Fori(1, NAH) as ah:
                    for r_ in range(2):
                        row_block(ah, r_)
                low_part(GB * NB - 1, GP - 1)
                dve.wait_ge(s_free, GB * NB + 2)
                nc.vector.tensor_reduce(den[:], acc[1][:, :, FOUT:HC], AX.X, ALU.add).then_inc(s_den, 1)
                dve.wait_ge(s_den, NB)
                nc.vector.reciprocal(rden[:], den[:]).then_inc(s_rden, 1)
                dve.wait_ge(s_xr, 16 * RT * NB)
                for u in range(RT):
                    dve.wait_ge(s_g, RT * (NB + 1) + u + 1)
                    nc.vector.tensor_tensor(y[:, u, :], y[:, u, :], x_res[:, u, :], ALU.add).then_inc(s_lasty, 1)
                    dve.wait_ge(s_lasty, u + 1)
                    nc.vector.bn_stats(stats[:, u, :], y[:, u, :]).then_inc(s_lastbn, 1)
                    dve.wait_ge(s_lastbn, u + 1)
                    nc.vector.bn_aggr(moments[:, u, :], stats[:, u, :]).then_inc(s_lastmv, 1)
                dve.wait_ge(s_lastmv, RT)
                nc.vector.tensor_scalar(var_e[:], moments[:, :, 1], EPS, None, ALU.add).then_inc(s_lastvar, 1)
                dve.wait_ge(s_lastrs, 1)
                nc.vector.scalar_tensor_tensor(out=bias[:], in0=moments[:, :, 0], scalar=-1.0, in1=rstd[:],
                                               op0=ALU.mult, op1=ALU.mult).then_inc(s_bias, 1)
                dve.wait_ge(s_bias, NB)
                for u in range(RT // 2, RT):
                    nc.vector.tensor_scalar(y[:, u, :], y[:, u, :], rstd[:, u:u + 1], bias[:, u:u + 1],
                                            ALU.mult, ALU.add).then_inc(s_lasto, 1)
            applies(dve, main)

        @block.tensor
        def _(pe):
            pe.sem_inc(s_xT, 4)
            pe.sem_inc(s_free, 2)
            pe.wait_ge(s_w, 32)
            pe.wait_ge(s_const, 2)
            for k in range(KT):
                for t in range(OT):
                    last = nc.tensor.transpose(ps_xT[k % 2][:, bass.ts(t, P)], w_in[:, t, bass.ts(k, P)], ident[:])
                last.then_inc(s_wT, 1)
            for k in range(KT):
                for t in range(OT):
                    last = nc.tensor.matmul(acc[1][:, 0, 2 * k:2 * k + 2], w_in[:, t, bass.ts(k, P)],
                                            r_in[:].rearrange("p (s t) -> p t s", t=OT)[:, t, :],
                                            start=(t == 0), stop=(t == OT - 1))
            last.then_inc(s_wr, 1)
            pe.wait_ge(s_wTc, KT + 1)

            def transpose_x(m, b):
                pe.wait_ge(s_x[b], 16 * m + 16)
                for r_ in range(2):
                    for k in range(KT):
                        last = nc.tensor.transpose(ps_xT[b % 2][:, bass.ts(KT * r_ + k, P)],
                                                   x_in[b][:, bass.ts(KT * r_ + k, P)], ident[:])
                last.then_inc(s_xT, 1)

            def wh_product(m, b):
                pe.wait_ge(s_xTc, 4 * m + (b + 1))
                for r_ in range(2):
                    pe.wait_ge(s_lo0, 8 * m + (2 * b + r_ + 1))
                    for k in range(KT):
                        last = nc.tensor.matmul(ps_wh[b % 2][:, r_, :], xT[:, b % 2, bass.ts(KT * r_ + k, P)],
                                                w_ext[:, k, :], start=(k == 0), stop=(k == KT - 1))
                last.then_inc(s_wh, 1)

            transpose_x(0, 0)
            transpose_x(0, 1)
            with pe.Fori(0, NC // 8 - 1) as m:
                for b in range(4):
                    wh_product(m, b)
                    transpose_x(*two_on(m, b))
            for b in range(4):
                wh_product(NC // 8 - 1, b)
                if b < 2:
                    transpose_x(NC // 8 - 1, b + 2)
            pe.wait_ge(s_Rc, 1)
            nc.tensor.transpose(acc[0][0:NC, 0, 0:P], Rc[:], ident[:]).then_inc(s_Rt, 1)

            def main():
                pe.wait_ge(s_vl, 1)
                pe.wait_ge(s_Rtc, 1)

                def piece(ah, r_, c, first=False, final=False):
                    for u in range(GP):
                        G = GB * (2 * ah + r_) + GP * c + u
                        pe.wait_ge(s_hi, G + 1)
                        for par in range(2):
                            k = CP * c + 2 * u + par
                            for v in range(RT):
                                nc.tensor.matmul(acc[r_][:, v, 0:HC], P_hi[:, u % 2, par, bass.ts(v, P)],
                                                 WV_hi[:, k, :], start=(first and u == 0 and par == 0),
                                                 stop=False)
                                nc.tensor.matmul(acc[r_][:, v, 0:FOUT], P_hi[:, u % 2, par, bass.ts(v, P)],
                                                 WV_lo[:, k, :], start=False, stop=False)
                        pe.wait_ge(s_lo, G + 1)
                        for par in range(2):
                            k = CP * c + 2 * u + par
                            for v in range(RT):
                                last = nc.tensor.matmul(acc[r_][:, v, 0:HC], P_lo[:, u % 2, par, bass.ts(v, P)],
                                                        WV_hi[:, k, :], start=False,
                                                        stop=(final and u == GP - 1 and par == 1))
                        last.then_inc(s_free, 1)

                with pe.Fori(0, NAH) as ah:
                    for r_ in range(2):
                        pe.wait_ge(s_g, 8 * ah + (4 * r_ + 4))
                        piece(ah, r_, 0, first=True)
                        with pe.Fori(1, PC - 1) as c:
                            piece(ah, r_, c)
                        piece(ah, r_, PC - 1, final=True)
            applies(pe, main)


def general_path(nc, x, adj, W, r, out, taken=None):
    N, FIN = x.shape
    FOUT = W.shape[0]
    NT = N // P
    KT = FIN // P
    OT = FOUT // P
    GRP = BANK // P
    NG = NT // GRP

    ctx = ExitStack()
    with ctx:
        def sb(name, shape, dt=F32):
            return ctx.enter_context(nc.sbuf_tensor("g_" + name, shape, dt))

        def pb(name, shape):
            return ctx.enter_context(nc.psum_tensor("g_" + name, shape, F32))

        def sem(name):
            return ctx.enter_context(nc.semaphore("g_" + name))

        ident = sb("ident", [P, P])
        ones = sb("ones", [P, P])
        w_in = sb("w_in", [P, OT, FIN])
        r_in = sb("r_in", [P, 2 * OT])
        w_ext = sb("w_ext", [P, KT, FOUT + 2])
        x_in = sb("x_in", [P, FIN])
        xT = sb("xT", [P, KT, P])
        Wh = sb("Wh", [P, NT, FOUT + 1])
        S = sb("S", [P, NT, 2])
        diag = sb("diag", [P, P])
        s_row = sb("s_row", [P, N])
        s_min = sb("s_min", [P, 1])
        A = sb("A", [P, N], I32)
        E = sb("E", [P, N])
        row_max = sb("row_max", [P, 3])
        ET = sb("ET", [P, 2, BANK])
        den = sb("den", [P, 1])
        xres = sb("xres", [P, FIN])
        h = sb("h", [P, FOUT])
        y = sb("y", [P, FOUT])
        o = sb("o", [P, FOUT])
        mv = sb("mv", [P, 2])
        rstd = sb("rstd", [P, 1])
        expo = sb("expo", [P, 1])
        ps_t = [pb(f"ps_t{i}", [P, BANK]) for i in range(2)]
        ps_a = pb("ps_a", [P, BANK])
        ps_b = pb("ps_b", [P, BANK])

        s_w = sem("w_loaded")
        s_const = sem("const_ready")
        s_wT = sem("w_transposed")
        s_wTc = sem("w_copied")
        s_wr = sem("w_r_product")
        s_ext = sem("w_ext_ready")
        s_x = sem("x_loaded")
        s_xT = sem("x_transposed")
        s_xTc = sem("x_copied")
        s_wh = sem("wh_product")
        s_whc = sem("wh_stored")
        s_dg = sem("diag_ready")
        s_bc = sem("row_broadcast")
        s_row_ok = sem("row_stored")
        s_dve = sem("vector_step")
        s_adj = sem("adj_loaded")
        s_lg = sem("logits_ready")
        s_exp = sem("exp_done")
        s_pm = sem("weights_masked")
        s_tr = sem("weights_transposed")
        s_cp = sem("transposed_copied")
        s_mm = sem("product_done")
        s_xr = sem("xres_loaded")
        s_h = sem("h_ready")
        s_g = sem("gelu_done")
        s_y = sem("variance_ready")
        s_rs = sem("rstd_ready")
        s_o = sem("out_ready")
        s_st = sem("out_stored")
        block = ctx.enter_context(nc.Block())

        def branch(eng, body):
            if taken is None:
                body()
            else:
                flag = eng.value_load(taken[0:1, 0:1], min_val=0, max_val=1)
                with eng.If(flag == 0):
                    body()

        @block.sync
        def _(sp):
            def body():
                for count in (s_st,):
                    sp.sem_inc(count, 1)
                sp.dma_start(w_in[:], W.rearrange("(t p) k -> p t k", p=P)).then_inc(s_w, 16)
                sp.dma_start(r_in[:], r.rearrange("(u p) a -> p (u a)", p=P),
                             allow_slow_non_contiguous=True).then_inc(s_w, 16)
                with sp.Fori(0, NT) as t:
                    sp.wait_ge(s_xT, t + 1)
                    sp.dma_start(x_in[:], x[bass.ts(t, P), :]).then_inc(s_x, 16)
                with sp.Fori(0, NT) as t:
                    sp.wait_ge(s_pm, t + 1)
                    sp.dma_start(A[:], adj[bass.ts(t, P), :]).then_inc(s_adj, 16)
                    sp.wait_ge(s_o, t + 1)
                    sp.dma_start(xres[:], x[bass.ts(t, P), :]).then_inc(s_xr, 16)
                    sp.wait_ge(s_o, t + 1 + 1)
                    sp.dma_start(out[bass.ts(t, P), :], o[:]).then_inc(s_st, 16)
                sp.wait_ge(s_st, 16 * NT + 1)
            branch(sp, body)

        @block.gpsimd
        def _(pool):
            def body():
                nc.gpsimd.memset(ident[:], 0.0).then_inc(s_const, 1)
                nc.gpsimd.memset(ones[:], 1.0).then_inc(s_const, 1)
                nc.gpsimd.memset(expo[:], -0.5).then_inc(s_const, 1)
                nc.gpsimd.memset(Wh[:, :, FOUT:FOUT + 1], 1.0).then_inc(s_const, 1)
                pool.wait_ge(s_const, 4)
                nc.gpsimd.affine_select(out=ident[:], in_=ident[:], compare_op=ALU.not_equal, fill=1.0,
                                        base=0, pattern=[[-1, P]], channel_multiplier=1).then_inc(s_const, 1)
                with pool.Fori(0, NT) as t:
                    pool.wait_ge(s_y, t + 1)
                    nc.gpsimd.tensor_tensor(rstd[:], mv[:, 1:2], expo[:], ALU.pow).then_inc(s_rs, 1)
            branch(pool, body)

        @block.scalar
        def _(act):
            def body():
                for count in (s_whc, s_row_ok, s_cp,):
                    act.sem_inc(count, 1)
                for g in range(KT):
                    act.wait_ge(s_wT, g + 1)
                    nc.scalar.copy(w_ext[:, g, 0:FOUT], ps_t[g % 2][:, 0:FOUT]).then_inc(s_wTc, 1)
                act.wait_ge(s_wr, 1)
                nc.scalar.copy(w_ext[:, :, FOUT:FOUT + 2],
                               ps_a[:, 0:2 * KT].rearrange("p (k c) -> p k c", c=2)).then_inc(s_ext, 1)
                with act.Fori(0, NT) as t:
                    act.wait_ge(s_xT, t + 1 + 1)
                    nc.scalar.copy(xT[:], ps_t[0][:, 0:FIN].rearrange("p (k m) -> p k m", m=P)).then_inc(s_xTc, 1)
                    act.wait_ge(s_wh, t + 1)
                    nc.scalar.copy(Wh[:, t, 0:FOUT], ps_a[:, 0:FOUT])
                    nc.scalar.copy(S[:, t, :], ps_a[:, FOUT:FOUT + 2]).then_inc(s_whc, 1)
                with act.Fori(0, NT) as t:
                    act.wait_ge(s_bc, t + 1 + 1)
                    nc.scalar.copy(s_row[:, bass.ts(t, P)], ps_b[:, 0:P]).then_inc(s_row_ok, 1)
                with act.Fori(0, NT) as t:
                    act.wait_ge(s_lg, t + 1)
                    nc.scalar.activation(E[:], E[:], ACT.Exp).then_inc(s_exp, 1)
                    for g in range(NG):
                        act.wait_ge(s_tr, NG * t + (g + 1) + 1)
                        if g >= 2:
                            act.wait_ge(s_mm, NG * t + (g - 1))
                        nc.scalar.copy(ET[:, g % 2, :], ps_t[g % 2][:]).then_inc(s_cp, 1)
                    act.wait_ge(s_h, t + 1 + 1)
                    nc.scalar.activation(y[:], h[:], ACT.Gelu).then_inc(s_g, 1)
            branch(act, body)

        @block.vector
        def _(dve):
            def body():
                for count in (s_pm, s_h, s_o,):
                    dve.sem_inc(count, 1)
                with dve.Fori(0, NT) as t:
                    dve.wait_ge(s_const, 5)
                    dve.wait_ge(s_whc, NT + 1)
                    dve.wait_ge(s_bc, t + 1)
                    nc.vector.tensor_scalar(diag[:], ident[:], S[:, t, 1:2], None, ALU.mult).then_inc(s_dg, 1)
                dve.wait_ge(s_row_ok, NT + 1)
                nc.vector.tensor_reduce(s_min[:], s_row[:], AX.X, ALU.min).then_inc(s_dve, 1)
                dve.wait_ge(s_dve, 1)
                with dve.Fori(0, NT) as t:
                    STEPS = 14
                    count = [0]

                    def link(ins):
                        count[0] += 1
                        ins.then_inc(s_dve, 1)
                        dve.wait_ge(s_dve, STEPS * t + (1 + count[0]))

                    dve.wait_ge(s_adj, 16 * t + 16)
                    dve.wait_ge(s_tr, NG * t + 1)
                    link(nc.vector.tensor_scalar(E[:], s_row[:], s_min[:], None, ALU.subtract))
                    link(nc.vector.scalar_tensor_tensor(out=E[:], in0=A[:], scalar=0.0, in1=E[:],
                                                        op0=ALU.not_equal, op1=ALU.mult))
                    link(nc.vector.tensor_reduce(row_max[:, 0:1], E[:], AX.X, ALU.max))
                    link(nc.vector.tensor_scalar(row_max[:, 1:2], row_max[:, 0:1], s_min[:], S[:, t, 0:1],
                                                 ALU.add, ALU.add))
                    link(nc.vector.scalar_tensor_tensor(out=row_max[:, 2:3], in0=row_max[:, 1:2], scalar=ALPHA,
                                                        in1=row_max[:, 1:2], op0=ALU.mult, op1=ALU.max))
                    link(nc.vector.tensor_scalar(E[:], s_row[:], S[:, t, 0:1], None, ALU.add))
                    link(nc.vector.scalar_tensor_tensor(out=E[:], in0=E[:], scalar=ALPHA, in1=E[:],
                                                        op0=ALU.mult, op1=ALU.max))
                    nc.vector.tensor_scalar(E[:], E[:], row_max[:, 2:3], 1.0, ALU.subtract, ALU.min).then_inc(s_lg, 1)
                    dve.wait_ge(s_exp, t + 1)
                    nc.vector.scalar_tensor_tensor(out=E[:], in0=A[:], scalar=0.0, in1=E[:],
                                                   op0=ALU.not_equal, op1=ALU.mult).then_inc(s_pm, 1)
                    dve.wait_ge(s_mm, NG * t + NG)
                    link(nc.vector.reciprocal(den[:], ps_a[:, FOUT:FOUT + 1]))
                    nc.vector.tensor_scalar(h[:], ps_a[:, 0:FOUT], den[:], None, ALU.mult).then_inc(s_h, 1)
                    dve.wait_ge(s_g, t + 1)
                    dve.wait_ge(s_xr, 16 * t + 16)
                    link(nc.vector.tensor_tensor(y[:], y[:], xres[:], ALU.add))
                    link(nc.vector.tensor_reduce(mv[:, 0:1], y[:], AX.X, ALU.add))
                    link(nc.vector.tensor_scalar(mv[:, 0:1], mv[:, 0:1], 1.0 / FOUT, None, ALU.mult))
                    link(nc.vector.tensor_scalar(y[:], y[:], mv[:, 0:1], None, ALU.subtract))
                    link(nc.vector.tensor_tensor(h[:], y[:], y[:], ALU.mult))
                    link(nc.vector.tensor_reduce(mv[:, 1:2], h[:], AX.X, ALU.add))
                    nc.vector.tensor_scalar(mv[:, 1:2], mv[:, 1:2], 1.0 / FOUT, EPS, ALU.mult, ALU.add).then_inc(s_y, 1)
                    dve.wait_ge(s_rs, t + 1)
                    dve.wait_ge(s_st, 16 * t + 1)
                    nc.vector.tensor_scalar(o[:], y[:], rstd[:], None, ALU.mult).then_inc(s_o, 1)
                    assert count[0] == STEPS
            branch(dve, body)

        @block.tensor
        def _(pe):
            def body():
                for count in (s_xT, s_bc, s_tr,):
                    pe.sem_inc(count, 1)
                pe.wait_ge(s_w, 32)
                pe.wait_ge(s_const, 5)
                for k in range(KT):
                    for t in range(OT):
                        last = nc.tensor.transpose(ps_t[k % 2][:, bass.ts(t, P)], w_in[:, t, bass.ts(k, P)], ident[:])
                    last.then_inc(s_wT, 1)
                for k in range(KT):
                    for t in range(OT):
                        last = nc.tensor.matmul(ps_a[:, 2 * k:2 * k + 2], w_in[:, t, bass.ts(k, P)], r_in[:].rearrange("p (s t) -> p t s", t=OT)[:, t, :],
                                                start=(t == 0), stop=(t == OT - 1))
                last.then_inc(s_wr, 1)
                pe.wait_ge(s_wTc, KT)
                pe.wait_ge(s_ext, 1)
                with pe.Fori(0, NT) as t:
                    pe.wait_ge(s_x, 16 * t + 16)
                    for k in range(KT):
                        last = nc.tensor.transpose(ps_t[0][:, bass.ts(k, P)], x_in[:, bass.ts(k, P)], ident[:])
                    last.then_inc(s_xT, 1)
                    pe.wait_ge(s_xTc, t + 1)
                    pe.wait_ge(s_whc, t + 1)
                    for k in range(KT):
                        last = nc.tensor.matmul(ps_a[:, 0:FOUT + 2], xT[:, k, :], w_ext[:, k, :],
                                                start=(k == 0), stop=(k == KT - 1))
                    last.then_inc(s_wh, 1)
                with pe.Fori(0, NT) as t:
                    pe.wait_ge(s_dg, t + 1)
                    pe.wait_ge(s_row_ok, t + 1)
                    nc.tensor.matmul(ps_b[:, 0:P], ones[:], diag[:], start=True, stop=True).then_inc(s_bc, 1)
                with pe.Fori(0, NT) as t:
                    pe.wait_ge(s_pm, t + 1 + 1)
                    pe.wait_ge(s_h, t + 1)
                    for g in range(NG + 1):
                        if g < NG:
                            if g < 2:
                                pe.wait_ge(s_cp, NG * t + 1)
                            else:
                                pe.wait_ge(s_cp, NG * t + (g - 1) + 1)
                            for i in range(GRP):
                                last = nc.tensor.transpose(ps_t[g % 2][:, bass.ts(i, P)],
                                                           E[:, bass.ts(g * GRP + i, P)], ident[:])
                            last.then_inc(s_tr, 1)
                        if g > 0:
                            pe.wait_ge(s_cp, NG * t + g + 1)
                            for i in range(GRP):
                                n = (g - 1) * GRP + i
                                last = nc.tensor.matmul(ps_a[:, 0:FOUT + 1], ET[:, (g - 1) % 2, bass.ts(i, P)],
                                                        Wh[:, n, :], start=(n == 0), stop=(n == NT - 1))
                            last.then_inc(s_mm, 1)
            branch(pe, body)


def layer(nc, x, adj, W, r, out):
    w_rows = nc.dram_tensor("w_rows", (x.shape[0] // BANK, BANK), F32).ap()
    with nc.sbuf_tensor("taken", [1, 1], I32) as taken:
        narrow_path(nc, x, adj, W, r, out, w_rows, taken)
        general_path(nc, x, adj, W, r, out, taken)


def kernel(**inputs):
    import numpy as np
    import concourse.bacc as bacc
    from concourse import mybir as mb
    from concourse.bass_utils import run_bass_kernel_spmd as run

    nc = bacc.Bacc("TRN2", target_bir_lowering=False, num_devices=1)
    arrays, args = {}, []
    for name in ("x", "adj", "L0_gnn_W", "L0_gnn_r"):
        a = np.ascontiguousarray(inputs[name])
        arrays[f"in_{name}"] = a
        args.append(nc.dram_tensor(f"in_{name}", a.shape, mb.dt.from_np(a.dtype), kind="ExternalInput").ap())
    out = nc.dram_tensor("out", inputs["x"].shape, mb.dt.float32, kind="ExternalOutput").ap()
    layer(nc, *args, out)
    got = run(nc, [arrays], core_ids=[0])
    return got.results[0]["out"]
```
